# Optimizing a Trainium2 kernel written in Bass

```python
import numpy as np
import jax
import jax.numpy as jnp

def _softmax(x, axis=-1):
    return jax.nn.softmax(x, axis=axis)

def _gelu(x):
    return jax.nn.gelu(x, approximate=True)

def _silu(x):
    return jax.nn.silu(x)

def _sigmoid(x):
    return jax.nn.sigmoid(x)

def _layernorm(x, axis=-1, eps=1e-05):
    m = jnp.mean(x, axis=axis, keepdims=True)
    v = jnp.var(x, axis=axis, keepdims=True)
    return (x - m) / jnp.sqrt(v + eps)

def _scatter_add(tgt, idx, src, axis=0):
    return tgt.at[idx].add(src)

def _segment_sum(src, seg, n):
    return jax.ops.segment_sum(src, seg, n)
kernel_name = 'mk_gnn_preln_d1_gnn_r64_739004'

def setup_inputs(seed: int=0):
    np.random.seed(seed)
    _w = jnp.asarray

    def _rec_inputs():
        import jax
        import jax.numpy as jnp
        _gk = jax.random.key(seed)
        x = -0.000202 + 1 * jax.random.normal(jax.random.fold_in(_gk, 1), (100000, 128), jnp.float32)
        _s = jax.random.randint(jax.random.fold_in(_gk, 2), (25000,), 0, 100000, jnp.int32)
        _d = jax.random.randint(jax.random.fold_in(_gk, 3), (25000,), 0, 100000, jnp.int32)
        _loop = jnp.arange(100000, dtype=jnp.int32)
        src = jnp.concatenate([_s, _d, _loop])
        dst = jnp.concatenate([_d, _s, _loop])
        _o = jnp.argsort(dst, stable=True)
        src = src[_o]
        dst = dst[_o]
        return (x, src, dst)
    x, src, dst = _rec_inputs()

    def _L0_gnn_setup():
        import jax, jax.numpy as jnp
        import numpy as np
        N_NODES = 50000
        N_EDGES = 12500
        D_IN, D_HID, D_OUT = (128, 256, 128)
        key = jax.random.key(seed)
        ks = jax.random.split(key, 12)
        s = lambda k, fi, fo: jax.random.normal(k, (fi, fo), jnp.float32) * (1.0 / np.sqrt(fi))
        return {'features': jax.random.normal(ks[0], (N_NODES, D_IN), jnp.float32), 'ws0': s(ks[1], D_IN, D_HID), 'wn0': s(ks[2], D_IN, D_HID), 'b0': jnp.zeros((D_HID,), jnp.float32), 'ws1': s(ks[3], D_HID, D_HID), 'wn1': s(ks[4], D_HID, D_HID), 'b1': jnp.zeros((D_HID,), jnp.float32), 'ws2': s(ks[5], D_HID, D_OUT), 'wn2': s(ks[6], D_HID, D_OUT), 'b2': jnp.zeros((D_OUT,), jnp.float32), 'src': jax.random.randint(ks[7], (N_EDGES,), 0, N_NODES, jnp.int32), 'dst': jax.random.randint(ks[8], (N_EDGES,), 0, N_NODES, jnp.int32)}
    _L0_gnn_all = _L0_gnn_setup()
    _L0_gnn_in = {k: v for k, v in _L0_gnn_all.items() if k in ('ws0', 'wn0', 'b0', 'ws1', 'wn1', 'b1', 'ws2', 'wn2', 'b2')}
    del _L0_gnn_all
    return {'x': x, 'src': src, 'dst': dst, 'L0_gnn_ws0': _L0_gnn_in['ws0'], 'L0_gnn_wn0': _L0_gnn_in['wn0'], 'L0_gnn_b0': _L0_gnn_in['b0'], 'L0_gnn_ws1': _L0_gnn_in['ws1'], 'L0_gnn_wn1': _L0_gnn_in['wn1'], 'L0_gnn_b1': _L0_gnn_in['b1'], 'L0_gnn_ws2': _L0_gnn_in['ws2'], 'L0_gnn_wn2': _L0_gnn_in['wn2'], 'L0_gnn_b2': _L0_gnn_in['b2']}

def reference(x, src, dst, L0_gnn_ws0, L0_gnn_wn0, L0_gnn_b0, L0_gnn_ws1, L0_gnn_wn1, L0_gnn_b1, L0_gnn_ws2, L0_gnn_wn2, L0_gnn_b2):
    import jax
    import jax.numpy as jnp

    def _L0_gnn_ref(features, ws0, wn0, b0, ws1, wn1, b1, ws2, wn2, b2, src, dst):
        import jax, jax.numpy as jnp
        import numpy as np
        N_NODES = 50000
        N_EDGES = 12500
        D_IN, D_HID, D_OUT = (128, 256, 128)
        n = features.shape[0]
        deg = jax.ops.segment_sum(jnp.ones_like(src, jnp.float32), dst, num_segments=n)
        inv_deg = jnp.where(deg > 0, 1.0 / jnp.maximum(deg, 1.0), 0.0)[:, None]

        def sage(h, w_self, w_neigh, b):
            agg = jax.ops.segment_sum(h[src], dst, num_segments=n) * inv_deg
            return h @ w_self + agg @ w_neigh + b
        h = jax.nn.relu(sage(features, ws0, wn0, b0))
        h = jax.nn.relu(sage(h, ws1, wn1, b1))
        h = sage(h, ws2, wn2, b2)
        return h
    h = jnp.maximum(_layernorm(x, axis=-1), 0.0)
    x = x + _L0_gnn_ref(h, L0_gnn_ws0, L0_gnn_wn0, L0_gnn_b0, L0_gnn_ws1, L0_gnn_wn1, L0_gnn_b1, L0_gnn_ws2, L0_gnn_wn2, L0_gnn_b2, src, dst)
    return x

_drawn_inputs = setup_inputs


def setup_inputs(seed=0):
    import zlib

    import numpy as np

    out = dict(_drawn_inputs(seed))
    spreads = {'L0_gnn_b0': (0.0, 0.1), 'L0_gnn_b1': (0.0, 0.1), 'L0_gnn_b2': (0.0, 0.1)}
    factors = {}
    for name, (base, spread) in spreads.items():
        noise = np.random.default_rng([zlib.crc32(name.encode()), seed]).standard_normal(out[name].shape)
        drawn = base * np.exp(spread * noise) if base else spread * noise
        out[name] = jnp.asarray(drawn.astype(out[name].dtype))
    for name, factor in factors.items():
        out[name] = (out[name] * factor).astype(out[name].dtype)
    return out
```

```python
import concourse.bass as bass
from concourse import mybir
from contextlib import ExitStack

FP32 = mybir.dt.float32
BF16 = mybir.dt.bfloat16
I32 = mybir.dt.int32
ALU = mybir.AluOpType
ACT = mybir.ActivationFunctionType
AX = mybir.AxisListType

P = 128
N_NODES = 100000
N_EDGES = 150000
D = 128
H = 256
PAIR = 2 * P
SLOTS = 4
PAIRS = -(-N_NODES // (PAIR * SLOTS)) * SLOTS
TILES = 2 * PAIRS
N_PAD = TILES * P
GROUP = 4 * P
GROUPS = N_PAD // GROUP
CHUNKS = 7
TP = TILES // CHUNKS
ROW = 120
ROWS = N_EDGES // ROW
WROWS = 3
WIN = WROWS * ROW
EP = 125
EW = N_EDGES // EP
SENTINEL = 1 << 20
EPS = 1e-5


class Step:

    def __init__(self, use, slot, total, looped):
        self.use, self.slot, self.total, self.looped = use, slot, total, looped
        self.n = use * SLOTS + slot if not looped or slot else use * SLOTS
        self.half = slot % 2

    def back(self, lag):
        at = self.slot - lag
        return Step(self.use + at // SLOTS if at // SLOTS else self.use, at % SLOTS, self.total, self.looped)

    def live(self):
        return self.looped or 0 <= self.n < self.total

    def has(self, earlier):
        return self.looped or self.n >= earlier


def pipeline(eng, step, total, lag):
    for n in range(2 * SLOTS):
        step(Step(n // SLOTS, n % SLOTS, total, False))
    with eng.Fori(2, total // SLOTS) as i:
        for slot in range(SLOTS):
            step(Step(i, slot, total, True))
    for n in range(total, total + lag):
        step(Step(n // SLOTS, n % SLOTS, total, False))


def build(nc, x, src, dst, ws0, wn0, b0, ws1, wn1, b1, ws2, wn2, b2, out):
    h0_dram = nc.dram_tensor("h0_rows", [N_PAD, D], FP32).ap()
    h1_dram = nc.dram_tensor("h1_rows", [N_PAD, H], FP32).ap()
    z_dram = nc.dram_tensor("z_rows", [N_PAD, D], FP32).ap()
    h0_sums = nc.dram_tensor("h0_sums", [N_PAD, D], FP32).ap()
    h1_sums = nc.dram_tensor("h1_sums", [N_PAD, H], FP32).ap()
    z_sums = nc.dram_tensor("z_sums", [N_PAD, D], FP32).ap()
    y_dram = nc.dram_tensor("y_rows", [N_PAD, D], FP32).ap()
    samples_dram = nc.dram_tensor("dst_samples", [EP, EW // ROW], FP32).ap()
    degree_dram = nc.dram_tensor("general_degrees", [N_PAD, 1], FP32).ap()

    src_rows = src.rearrange("(r w) -> r w", w=ROW)
    dst_rows = dst.rearrange("(r w) -> r w", w=ROW)
    src_flat = src.rearrange("(p w) -> p w", w=EW)
    dst_flat = dst.rearrange("(p w) -> p w", w=EW)

    with ExitStack() as ctx:
        def sb(name, shape, dt=FP32):
            return ctx.enter_context(nc.sbuf_tensor(name, shape, dt))

        def sem(name):
            return ctx.enter_context(nc.semaphore(name))

        def sems(name, n=SLOTS):
            return [sem(f"{name}{i}") for i in range(n)]

        iota_row = sb("iota_row", [P, P])
        iota_col = sb("iota_col", [P, 1])
        iota_row_i = sb("iota_row_i", [P, P], I32)
        iota_col_i = sb("iota_col_i", [P, 1], I32)
        ident = sb("ident", [P, P])
        ones = sb("ones", [P, P])
        ones3 = sb("ones3", [3, P], BF16)
        eps_col = sb("eps_col", [P, 1])
        w0 = sb("w0", [P, 2, H])
        w1 = sb("w1", [P, 4, H])
        w2 = sb("w2", [P, 2, 2 * D])
        b1_col = sb("b1_col", [P, 2])
        bias_row = sb("bias_row", [1, H + D])
        bias_rest = sb("bias_rest", [1, 2, H + D])
        bias_part = sb("bias_part", [1, 3, H + D], BF16)
        bias3 = sb("bias3", [3, H + D], BF16)

        slot_index = sb("slot_index", [P, TILES], I32)
        slot_node = sb("slot_node", [P, TILES])
        base_degree = sb("base_degree", [P, TILES])
        inv_degree = sb("inv_degree", [P, TILES])
        self_scale = sb("self_scale", [P, TILES])
        fast = sb("fast", [P, 1])
        general_flag = sb("general_flag", [1, 1], I32)

        layer_mem = sb("layer_mem", [P, 12800])
        taken = [0]

        def part(a, b):
            at = taken[0]
            taken[0] += a * b
            assert taken[0] <= 12800
            return layer_mem[:, at:at + a * b].rearrange("p (a b) -> p a b", a=a)

        dst_all = sb("dst_all", [EP, EW], I32)
        dst_next = sb("dst_next", [EP - 1, 2], I32)
        samples = sb("samples", [EP, EW // ROW])
        samples_b = sb("samples_b", [TP, ROWS])
        scratch_rows = sb("scratch_rows", [P, ROWS])
        tile_base_i = sb("tile_base_i", [TP, CHUNKS], I32)
        tile_base = sb("tile_base", [TP, CHUNKS])
        below = sb("below", [TP, CHUNKS])
        row_f = sb("row_f", [TP, CHUNKS])
        row_index = sb("row_index", [TP, WROWS, CHUNKS], I32)
        win_dst = sb("win_dst", [TP, CHUNKS, WIN], I32)
        win_src = sb("win_src", [TP, CHUNKS, WIN], I32)
        wf_dst, wf_src, wf_rel, wf_in, wf_loop = (
            layer_mem[0:TP, i * CHUNKS * WIN:(i + 1) * CHUNKS * WIN].rearrange("p (c w) -> p c w", c=CHUNKS)
            for i in range(5))
        wf_key = sb("wf_key", [TP, CHUNKS, WIN])
        loop_count = sb("loop_count", [TP, CHUNKS])
        nodes_in = sb("nodes_in", [TP, CHUNKS])
        top8 = sb("top8", [TP, CHUNKS, 8])
        keys = sb("keys", [TP, CHUNKS, P])
        keys_t = sb("keys_t", [P, TILES])
        empty_t = sb("empty_t", [P, TILES])
        key_i = sb("key_i", [P, TILES], I32)
        node_i = sb("node_i", [P, TILES], I32)
        faults = sb("faults", [P, 8])
        fault_sum = sb("fault_sum", [P, 1])

        xg = [sb(f"xg{i}", [P, 4, D]) for i in range(SLOTS)]
        h0g = [sb(f"h0g{i}", [P, 4, D]) for i in range(SLOTS)]
        stats = [sb(f"stats{i}", [P, 4, 6]) for i in range(2)]
        moments = [sb(f"moments{i}", [P, 4, 2]) for i in range(2)]
        std = [sb(f"std{i}", [P, 4]) for i in range(2)]
        rstd = [sb(f"rstd{i}", [P, 4]) for i in range(2)]
        shift = [sb(f"shift{i}", [P, 4]) for i in range(2)]

        own = [part(2, H) for i in range(SLOTS)]
        nbr = [sb(f"nbr{i}", [P, 2, H]) for i in range(SLOTS)]
        gather_at = [sb(f"gather_at{i}", [P, 2], I32) for i in range(SLOTS)]
        select = [sb(f"select{i}", [P, 2, P]) for i in range(2)]
        degree = [sb(f"degree{i}", [P, 2]) for i in range(2)]
        own_scaled = [part(2, H) for i in range(2)]
        agg = [part(2, H) for i in range(2)]
        cat_t = [part(4, PAIR) for i in range(2)]
        h2_t = [part(2, PAIR) for i in range(2)]
        h1_out = [part(2, H) for i in range(SLOTS)]
        z_out = [part(2, D) for i in range(SLOTS)]
        y_mid = [part(2, D) for i in range(2)]
        y_out = [part(2, D) for i in range(SLOTS)]
        x_in = [part(2, D) for i in range(SLOTS)]

        src_all = sb("src_all", [EP, EW], I32)
        zero_rows = sb("zero_rows", [P, 4 * H])
        ge_src = sb("ge_src", [EP, 1], I32)
        ge_at = sb("ge_at", [EP, 1], I32)
        ge_put_at = sb("ge_put_at", [EP, 1], I32)
        ge_dst = sb("ge_dst", [EP, 1])
        ge_dst_b = sb("ge_dst_b", [EP, EP])
        ge_same = sb("ge_same", [EP, EP])
        ge_before = sb("ge_before", [EP, EP])
        ge_mask = sb("ge_mask", [EP, EP])
        ge_dup = sb("ge_dup", [EP, 1])
        ge_count = sb("ge_count", [EP, 1])
        ge_msg = sb("ge_msg", [EP, H])
        ge_cur = sb("ge_cur", [EP, H])
        ge_new = sb("ge_new", [EP, H])
        ge_deg = sb("ge_deg", [EP, 1])
        ge_deg_new = sb("ge_deg_new", [EP, 1])
        ge_base = sb("ge_base", [P, TILES])

        ps = {k: [ctx.enter_context(nc.psum_tensor(f"ps_{k}{i}", [P, 512], FP32)) for i in range(2)]
              for k in ("agg", "turn", "hid", "out")}

        w_loaded, bias_moved = sem("w_loaded"), sem("bias_moved")
        iota_made, const_made = sem("iota_made"), sem("const_made")
        bias_split = sem("bias_split")
        dst_loaded, sampled, sample_stored, sample_spread = (
            sem("dst_loaded"), sem("sampled"), sem("sample_stored"), sem("sample_spread"))
        rows_found, win_cleared, win_gathered = sem("rows_found"), sem("win_cleared"), sem("win_gathered")
        prep = sem("prep")
        keys_ready, keys_turned = sem("keys_ready"), sem("keys_turned")
        faults_ready, faults_summed, flag_set = sem("faults_ready"), sem("faults_summed"), sem("flag_set")
        tables_ready = sem("tables_ready")
        nbr_cleared = sem("nbr_cleared")

        x_loaded, stats_done, moments_ready = sems("x_loaded"), sem("stats_done"), sem("moments_ready")
        std_ready, recip_done, norm_ready = sem("std_ready"), sem("recip_done"), sem("norm_ready")
        h0_ready, h0_stored = sem("h0_ready"), sems("h0_stored")

        class Layer:

            def __init__(self, n):
                self.own_loaded = sems(f"own_loaded_{n}_")
                self.x_loaded = sems(f"x_in_loaded_{n}_")
                self.index_copied = sem(f"index_copied_{n}")
                self.gathered = sems(f"gathered_{n}_")
                self.selected = sem(f"selected_{n}")
                self.summed = sem(f"summed_{n}")
                self.degree_done = sem(f"degree_done_{n}")
                self.recip_done = sem(f"inv_degree_done_{n}")
                self.scale_ready = sem(f"scale_ready_{n}")
                self.own_scaled = sem(f"own_scaled_{n}_done")
                self.agg_ready = sem(f"agg_ready_{n}")
                self.turned = sem(f"turned_{n}")
                self.cat_ready = sem(f"cat_ready_{n}")
                self.cat_ready_act = sem(f"cat_ready_act_{n}")
                self.hid_done = sem(f"hid_done_{n}")
                self.h2_ready = sem(f"h2_ready_{n}")
                self.dense_done = sem(f"dense_done_{n}")
                self.z_ready = sem(f"z_ready_{n}")
                self.y_mid_ready = sem(f"y_mid_ready_{n}")
                self.rows_ready = sem(f"rows_ready_{n}")
                self.stored = sems(f"stored_{n}_")

        sp_may_load = sem("sp_may_load")
        pool_may_go = sem("pool_may_go")

        L0, L1, L2 = Layer(0), Layer(1), Layer(2)

        ge_loaded, ge_zeroed = sem("ge_loaded"), sem("ge_zeroed")
        ge_dve, ge_spread, ge_turned, ge_index = sem("ge_dve"), sem("ge_spread"), sem("ge_turned"), sem("ge_index")
        ge_fetched, ge_summed, ge_new_ready, ge_put = (
            sem("ge_fetched"), sem("ge_summed"), sem("ge_new_ready"), sem("ge_put"))
        ge_zero_made, ge_base_loaded, ge_tables = sem("ge_zero_made"), sem("ge_base_loaded"), sem("ge_tables")
        ge_done = sem("ge_done")

        def pair_rows(table, s):
            return table[bass.ds(s.n * PAIR, PAIR), :].rearrange("(j p) f -> p j f", p=P)

        def group_rows(table, s):
            return table[bass.ds(s.n * GROUP, GROUP), :].rearrange("(j p) f -> p j f", p=P)

        def all_stored(eng, stored, per_slot):
            for q in range(SLOTS):
                eng.wait_ge(stored[q], per_slot * 16)

        SLOT_USES = PAIRS // SLOTS
        GENERAL = [(h0_dram, h0_sums, D), (h1_dram, h1_sums, H), (z_dram, z_sums, D)]
        ZERO_ROWS = 4 * P

        block = ctx.enter_context(nc.Block())

        @block.sync
        def _(sp):
            sp.dma_start(dst_all[:, :], dst_flat).then_inc(dst_loaded, 16)
            sp.dma_start(dst_next[:, :], dst_flat[1:EP, 0:2]).then_inc(dst_loaded, 16)
            sp.dma_start(bias_row[:, 0:H], b0.rearrange("(a n) -> a n", a=1)).then_inc(w_loaded, 16)
            sp.dma_start(bias_row[:, H:H + D], b2.rearrange("(a n) -> a n", a=1)).then_inc(w_loaded, 16)
            sp.dma_start(b1_col[:, :], b1.rearrange("(m p) -> p m", p=P), allow_slow_non_contiguous=True).then_inc(w_loaded, 16)
            sp.dma_start(w0[:, 0, :], ws0).then_inc(w_loaded, 16)
            sp.dma_start(w0[:, 1, :], wn0).then_inc(w_loaded, 16)
            sp.dma_start(w1[:, 0:2, :], ws1.rearrange("(k p) n -> p k n", p=P)).then_inc(w_loaded, 16)
            sp.dma_start(w1[:, 2:4, :], wn1.rearrange("(k p) n -> p k n", p=P)).then_inc(w_loaded, 16)
            sp.dma_start(w2[:, :, 0:D], wn2.rearrange("(k p) n -> p k n", p=P)).then_inc(w_loaded, 16)
            sp.dma_start(w2[:, :, D:2 * D], ws2.rearrange("(k p) n -> p k n", p=P)).then_inc(w_loaded, 16)
            sp.wait_ge(sampled, 1)
            sp.dma_start(samples_dram, samples[:, :]).then_inc(sample_stored, 16)
            sp.wait_ge(sample_stored, 16)
            sp.dma_start(samples_b[:, :], samples_dram.rearrange("(a p) w -> a (p w)", a=1).to_broadcast([TP, ROWS])
                         ).then_inc(sample_spread, 16)
            sp.wait_ge(bias_split, 5)
            for part in range(3):
                sp.dma_start(bias3[part:part + 1, :], bias_part[:, part, :]).then_inc(bias_moved, 16)

            def load_x(s):
                if not s.live():
                    return
                if s.has(SLOTS):
                    sp.wait_ge(h0_ready, s.back(SLOTS).n + 1)
                    sp.sem_inc(sp_may_load, 1)
                sp.dma_start(xg[s.slot][:, :, :], group_rows(x, s)).then_inc(x_loaded[s.slot], 16)
            pipeline(sp, load_x, GROUPS, 0)

            def general(pass_no):
                table, sums, width = GENERAL[pass_no]
                with sp.If(sp.value_load(general_flag[0:1, 0:1], min_val=0, max_val=1) != 0):
                    if pass_no == 0:
                        sp.dma_start(src_all[:, :], src_flat).then_inc(ge_loaded, 16)
                        sp.wait_ge(ge_zero_made, 1)
                        sp.dma_start(degree_dram.rearrange("(a p c) o -> a p (c o)", a=1, p=P)[0],
                                     zero_rows[:, 0:TILES]).then_inc(ge_zeroed, 16)
                        sp.wait_ge(ge_zeroed, 16)
                    done = [1, 1 + GROUPS, 1 + 2 * GROUPS][pass_no]
                    with sp.Fori(0, GROUPS) as i:
                        sp.dma_start(sums[bass.ds(i * ZERO_ROWS, ZERO_ROWS), :]
                                     .rearrange("(p j) f -> p (j f)", p=P),
                                     zero_rows[:, 0:4 * width]).then_inc(ge_zeroed, 16)
                        sp.wait_ge(ge_zeroed, i * 16 + (done + 1) * 16)
                        sp.sem_inc(sp_may_load, 1)
                    sp.sem_inc(ge_done, 1)
                    if pass_no == 0:
                        sp.wait_ge(ge_put, 16 * 2 * EW)
                        sp.dma_start(ge_base[:, :], degree_dram.rearrange("(t p) o -> p (t o)", p=P),
                                     allow_slow_non_contiguous=True
                                     ).then_inc(ge_base_loaded, 16)

            def load_own(layer, table, width, s, freed):
                if not s.live():
                    return
                if s.has(SLOTS):
                    sp.wait_ge(freed, s.back(SLOTS).n + 1)
                    sp.sem_inc(sp_may_load, 1)
                sp.dma_start(own[s.slot][:, :, 0:width], pair_rows(table, s)).then_inc(layer.own_loaded[s.slot], 16)

            sp.wait_ge(flag_set, 1)
            all_stored(sp, h0_stored, GROUPS // SLOTS)
            general(0)
            pipeline(sp, lambda s: load_own(L0, h0_dram, D, s, L0.turned), PAIRS, 0)

            all_stored(sp, L0.stored, SLOT_USES)
            general(1)

            def layer1_loads(s):
                load_own(L1, h1_dram, H, s, L1.turned)
                t = s.back(2)
                if t.live():
                    if t.has(SLOTS):
                        sp.wait_ge(L1.rows_ready, t.back(SLOTS).n + 1)
                        sp.sem_inc(sp_may_load, 1)
                    sp.dma_start(x_in[t.slot][:, :, :], pair_rows(x, t)).then_inc(L1.x_loaded[t.slot], 16)
            pipeline(sp, layer1_loads, PAIRS, 2)

            all_stored(sp, L1.stored, 2 * SLOT_USES)
            general(2)
            pipeline(sp, lambda s: load_own(L2, y_dram, D, s, L2.rows_ready), PAIRS, 0)
            all_stored(sp, L2.stored, SLOT_USES)

        @block.gpsimd
        def _(pool):
            pool.iota(iota_row_i[:, :], pattern=[[1, P]], base=0, channel_multiplier=0).then_inc(iota_made, 1)
            pool.iota(iota_col_i[:, :], pattern=[[0, 1]], base=0, channel_multiplier=1).then_inc(iota_made, 1)
            pool.iota(tile_base_i[:, :], pattern=[[P * TP, CHUNKS]], base=0, channel_multiplier=P
                      ).then_inc(iota_made, 1)
            pool.memset(win_dst[:, :, :], SENTINEL).then_inc(win_cleared, 1)
            pool.memset(win_src[:, :, :], 0).then_inc(win_cleared, 1)
            for q in range(SLOTS):
                pool.memset(nbr[q][:, :, :], 0.0).then_inc(nbr_cleared, 1)
            pool.wait_ge(nbr_cleared, SLOTS)
            for q in range(SLOTS):
                pool.memset(nbr[q][:, :, D:D + 1], 1.0).then_inc(nbr_cleared, 1)
            pool.wait_ge(win_cleared, 2)
            pool.wait_ge(rows_found, 1)
            for c in range(CHUNKS):
                for r in range(WROWS):
                    for rows, win in ((dst_rows, win_dst), (src_rows, win_src)):
                        pool.indirect_dma_start(win[:, c, r * ROW:(r + 1) * ROW], None, rows,
                                                bass.IndirectOffsetOnAxis(row_index[:, r, c:c + 1], axis=0),
                                                bounds_check=ROWS - 1, oob_is_err=False).then_inc(win_gathered, 16)

            limit = pool.alloc_register("last_row")
            pool.reg_mov(limit, N_PAD - 1)
            last_row = pool.snap(limit)

            def general(pass_no):
                table, sums, width = GENERAL[pass_no]
                with pool.If(pool.value_load(general_flag[0:1, 0:1], min_val=0, max_val=1) != 0):
                    if pass_no == 0:
                        pool.memset(zero_rows[:, :], 0.0).then_inc(ge_zero_made, 1)
                        pool.iota(slot_index[:, :], pattern=[[P, TILES]], base=0, channel_multiplier=1
                                  ).then_inc(ge_tables, 1)
                    pool.wait_ge(ge_done, 2 * pass_no + 1)
                    with_degree = pass_no == 0
                    fetched, put = ([0, 3, 5][pass_no] * EW, [0, 2, 3][pass_no] * EW)
                    fetches, puts = (3, 2) if with_degree else (2, 1)
                    with pool.Fori(0, EW) as i:
                        pool.wait_ge(ge_index, i + (pass_no * EW + 1))
                        pool.sem_inc(pool_may_go, 1)
                        pool.indirect_dma_start(ge_msg[:, 0:width], None, table,
                                                bass.IndirectOffsetOnAxis(ge_src[:, :], axis=0),
                                                bounds_check=last_row, oob_is_err=False).then_inc(ge_fetched, 16)
                        pool.indirect_dma_start(ge_cur[:, 0:width], None, sums,
                                                bass.IndirectOffsetOnAxis(ge_at[:, :], axis=0),
                                                bounds_check=last_row, oob_is_err=False).then_inc(ge_fetched, 16)
                        if with_degree:
                            pool.indirect_dma_start(ge_deg[:, :], None, degree_dram,
                                                    bass.IndirectOffsetOnAxis(ge_at[:, :], axis=0),
                                                    bounds_check=N_PAD - 1, oob_is_err=False
                                                    ).then_inc(ge_fetched, 16)
                        pool.wait_ge(ge_new_ready, i + (pass_no * EW + 1))
                        pool.sem_inc(pool_may_go, 1)
                        pool.indirect_dma_start(sums, bass.IndirectOffsetOnAxis(ge_put_at[:, :], axis=0),
                                                ge_new[:, 0:width], None,
                                                bounds_check=last_row, oob_is_err=False).then_inc(ge_put, 16)
                        if with_degree:
                            pool.indirect_dma_start(degree_dram, bass.IndirectOffsetOnAxis(ge_put_at[:, :], axis=0),
                                                    ge_deg_new[:, :], None,
                                                    bounds_check=N_PAD - 1, oob_is_err=False).then_inc(ge_put, 16)
                        pool.wait_ge(ge_put, i * (16 * puts) + 16 * (put + puts))
                        pool.sem_inc(pool_may_go, 1)
                    if pass_no == 0:
                        pool.wait_ge(ge_tables, 1)

            def gathers(layer, table, width):
                def copy_index(s):
                    if not s.live():
                        return
                    if s.has(SLOTS):
                        pool.wait_ge(layer.gathered[s.slot], s.use * 32)
                    pool.sem_inc(pool_may_go, 1)
                    pool.tensor_copy(gather_at[s.slot][:, :], slot_index[:, bass.ds(s.n * 2, 2)]
                                     ).then_inc(layer.index_copied, 1)

                def gather(s):
                    if not s.live():
                        return
                    if s.has(SLOTS):
                        pool.wait_ge(layer.summed, s.back(SLOTS).n + 1)
                    pool.wait_ge(layer.index_copied, s.n + 1)
                    pool.sem_inc(pool_may_go, 1)
                    for j in range(2):
                        pool.indirect_dma_start(nbr[s.slot][:, j, 0:width], None, table,
                                                bass.IndirectOffsetOnAxis(gather_at[s.slot][:, j:j + 1], axis=0),
                                                bounds_check=last_row, oob_is_err=False
                                                ).then_inc(layer.gathered[s.slot], 16)

                def step(s):
                    copy_index(s)
                    gather(s.back(1))
                pipeline(pool, step, PAIRS, 1)

            def gather_pass(layer, pass_no):
                table, sums, width = GENERAL[pass_no]
                with pool.If(pool.value_load(general_flag[0:1, 0:1], min_val=0, max_val=1) != 0):
                    gathers(layer, sums, width)
                with pool.Else():
                    gathers(layer, table, width)

            pool.wait_ge(flag_set, 1)
            pool.wait_ge(tables_ready, 1)
            all_stored(pool, h0_stored, GROUPS // SLOTS)
            pool.wait_ge(nbr_cleared, 2 * SLOTS)
            general(0)
            gather_pass(L0, 0)
            all_stored(pool, L0.stored, SLOT_USES)
            general(1)
            gather_pass(L1, 1)
            all_stored(pool, L1.stored, 2 * SLOT_USES)
            general(2)
            gather_pass(L2, 2)

        @block.scalar
        def _(act):
            act.wait_ge(const_made, 1)

            def norm_step(s):
                if s.live():
                    act.wait_ge(moments_ready, s.n + 1)
                    if s.has(2):
                        act.wait_ge(norm_ready, s.back(2).n + 1)
                    act.activation(std[s.half][:, :], moments[s.half][:, :, 1], ACT.Sqrt, bias=eps_col[:, :]
                                   ).then_inc(std_ready, 1)
                t = s.back(1)
                if t.live():
                    act.wait_ge(norm_ready, t.n + 1)
                    act.wait_ge(x_loaded[t.slot], (t.use + 1) * 16)
                    if t.has(SLOTS):
                        act.wait_ge(h0_stored[t.slot], t.use * 16)
                    for j in range(4):
                        last = act.activation(h0g[t.slot][:, j, :], xg[t.slot][:, j, :], ACT.Relu,
                                              bias=shift[t.half][:, j:j + 1], scale=rstd[t.half][:, j:j + 1])
                    last.then_inc(h0_ready, 1)
                u = s.back(2)
                if u.live():
                    act.wait_ge(h0_ready, u.n + 1)
                    act.dma_start(group_rows(h0_dram, u), h0g[u.slot][:, :, :]).then_inc(h0_stored[u.slot], 16)
            pipeline(act, norm_step, GROUPS, 2)

            def scale_own(layer, s, width):
                if not s.live():
                    return
                act.wait_ge(layer.own_loaded[s.slot], (s.use + 1) * 16)
                if layer is L0:
                    act.wait_ge(L0.scale_ready, s.n + 1)
                if s.has(2):
                    act.wait_ge(layer.agg_ready, s.back(2).n + 1)
                for j in range(2):
                    last = act.activation(own_scaled[s.half][:, j, 0:width], own[s.slot][:, j, 0:width], ACT.Copy,
                                          scale=self_scale[:, bass.ds(s.n * 2 + j, 1)])
                last.then_inc(layer.own_scaled, 1)

            def layer0(s):
                scale_own(L0, s, D)
                t = s.back(2)
                if t.live():
                    act.wait_ge(L0.dense_done, t.n + 1)
                    if t.has(SLOTS):
                        act.wait_ge(L0.stored[t.slot], t.use * 16)
                    act.activation(h1_out[t.slot][:, :, :], ps["out"][t.half][:, :].rearrange("p (j f) -> p j f", j=2),
                                   ACT.Relu).then_inc(L0.rows_ready, 1)
                u = s.back(3)
                if u.live():
                    act.wait_ge(L0.rows_ready, u.n + 1)
                    act.dma_start(pair_rows(h1_dram, u), h1_out[u.slot][:, :, :]).then_inc(L0.stored[u.slot], 16)
            pipeline(act, layer0, PAIRS, 3)

            def layer1(s):
                scale_own(L1, s, H)
                t = s.back(1)
                if t.live():
                    act.wait_ge(L1.turned, t.n + 1)
                    if t.has(2):
                        act.wait_ge(L1.hid_done, t.back(2).n + 1)
                    act.activation(cat_t[t.half][:, :, P:PAIR], ps["turn"][1][:, :].rearrange("p (k n) -> p k n", k=4),
                                   ACT.Copy).then_inc(L1.cat_ready_act, 1)
                t = s.back(2)
                if t.live():
                    act.wait_ge(L1.hid_done, t.n + 1)
                    if t.has(2):
                        act.wait_ge(L1.dense_done, t.back(2).n + 1)
                    for m in range(2):
                        last = act.activation(h2_t[t.half][:, m, :], ps["hid"][t.half][:, m * PAIR:(m + 1) * PAIR],
                                              ACT.Relu, bias=b1_col[:, m:m + 1])
                    last.then_inc(L1.h2_ready, 1)
                t = s.back(3)
                if t.live():
                    act.wait_ge(L1.dense_done, t.n + 1)
                    if t.has(SLOTS):
                        act.wait_ge(L1.stored[t.slot], t.use * 32)
                    act.activation(z_out[t.slot][:, :, :],
                                   ps["out"][t.half][:, :].rearrange("p (j f) -> p j f", j=2)[:, :, 0:D],
                                   ACT.Copy).then_inc(L1.z_ready, 1)
                u = s.back(4)
                if u.live():
                    act.wait_ge(L1.rows_ready, u.n + 1)
                    act.dma_start(pair_rows(z_dram, u), z_out[u.slot][:, :, :]).then_inc(L1.stored[u.slot], 16)
                    act.dma_start(pair_rows(y_dram, u), y_out[u.slot][:, :, :]).then_inc(L1.stored[u.slot], 16)
            pipeline(act, layer1, PAIRS, 4)

            def layer2(s):
                u = s.back(1)
                if u.live():
                    act.wait_ge(L2.rows_ready, u.n + 1)
                    act.dma_start(pair_rows(out, u), y_out[u.slot][:, :, :]).then_inc(L2.stored[u.slot], 16)
            pipeline(act, layer2, PAIRS, 1)

        @block.vector
        def _(dve):
            dve.wait_ge(iota_made, 3)
            dve.tensor_copy(iota_row[:, :], iota_row_i[:, :])
            dve.tensor_copy(iota_col[:, :], iota_col_i[:, :])
            dve.tensor_copy(tile_base[:, :], tile_base_i[:, :])
            dve.memset(ones[:, :], 1.0)
            dve.memset(ones3[:, :], 1.0)
            dve.memset(faults[:, :], 0.0)
            dve.memset(base_degree[:, :], 1.0)
            dve.memset(eps_col[:, :], EPS).then_inc(const_made, 1)
            dve.wait_ge(const_made, 1)
            dve.tensor_scalar(ident[:, :], iota_row[:, :], iota_col[:, 0:1], None, op0=ALU.is_equal
                              ).then_inc(const_made, 1)
            done = [0]

            def own_step(ins):
                done[0] += 1
                ins.then_inc(prep, 1)
                dve.wait_ge(prep, done[0])

            dve.wait_ge(dst_loaded, 32)
            dve.tensor_copy(samples[:, :], dst_all[:, :].rearrange("p (r w) -> p r w", w=ROW)[:, :, 0]
                            ).then_inc(sampled, 1)
            own_step(dve.tensor_tensor(scratch_rows[0:EP, 0:EW - 1], dst_all[:, 0:EW - 1], dst_all[:, 1:EW],
                                       ALU.is_gt))
            dve.reduce_sum(faults[0:EP, 0:1], scratch_rows[0:EP, 0:EW - 1], AX.X)
            own_step(dve.tensor_tensor(faults[0:EP - 1, 1:2], dst_all[0:EP - 1, EW - 1:EW], dst_next[:, 0:1], ALU.is_gt))

            dve.wait_ge(w_loaded, 16 * 9)
            dve.tensor_copy(bias_part[:, 0, :], bias_row[:, :]).then_inc(bias_split, 1)
            dve.wait_ge(bias_split, 1)
            dve.tensor_tensor(bias_rest[:, 0, :], bias_row[:, :], bias_part[:, 0, :], ALU.subtract).then_inc(bias_split, 1)
            dve.wait_ge(bias_split, 2)
            dve.tensor_copy(bias_part[:, 1, :], bias_rest[:, 0, :]).then_inc(bias_split, 1)
            dve.wait_ge(bias_split, 3)
            dve.tensor_tensor(bias_rest[:, 1, :], bias_rest[:, 0, :], bias_part[:, 1, :], ALU.subtract
                              ).then_inc(bias_split, 1)
            dve.wait_ge(bias_split, 4)
            dve.tensor_copy(bias_part[:, 2, :], bias_rest[:, 1, :]).then_inc(bias_split, 1)

            dve.wait_ge(sample_spread, 16)
            for c in range(CHUNKS):
                own_step(dve.tensor_scalar(scratch_rows[0:TP, :], samples_b[:, :], tile_base[:, c:c + 1], None,
                                           op0=ALU.is_lt, op1=ALU.add, accum_out=below[:, c:c + 1]))
            own_step(dve.tensor_scalar(row_f[:, :], below[:, :], -1.0, 0.0, op0=ALU.add, op1=ALU.max))
            for r in range(WROWS):
                last = dve.tensor_scalar(row_index[:, r, :], row_f[:, :], float(r), None, op0=ALU.add)
            last.then_inc(rows_found, 1)

            wide = [TP, CHUNKS, WIN]
            base_b = tile_base[:, :].rearrange("p (c a) -> p c a", a=1).to_broadcast(wide)
            dve.wait_ge(win_gathered, 16 * CHUNKS * WROWS * 2)
            dve.tensor_copy(wf_dst[:, :, :], win_dst[:, :, :])
            own_step(dve.tensor_copy(wf_src[:, :, :], win_src[:, :, :]))
            own_step(dve.tensor_tensor(wf_rel[:, :, :], wf_dst[:, :, :], base_b, ALU.subtract))
            own_step(dve.tensor_scalar(wf_in[:, :, :], wf_rel[:, :, :], 0.0, None, op0=ALU.is_ge))
            own_step(dve.scalar_tensor_tensor(wf_in[:, :, :], wf_rel[:, :, :], float(P), wf_in[:, :, :],
                                              op0=ALU.is_lt, op1=ALU.mult))
            dve.memset(wf_loop[:, :, WIN - 1:WIN], 0.0)
            own_step(dve.tensor_tensor(wf_loop[:, :, 0:WIN - 1], wf_dst[:, :, 0:WIN - 1], wf_dst[:, :, 1:WIN],
                                       ALU.not_equal))
            own_step(dve.tensor_tensor(wf_key[:, :, :], wf_src[:, :, :], wf_dst[:, :, :], ALU.is_equal))
            own_step(dve.tensor_tensor(wf_loop[:, :, :], wf_loop[:, :, :], wf_key[:, :, :], ALU.mult))
            own_step(dve.tensor_tensor(wf_loop[:, :, :], wf_loop[:, :, :], wf_in[:, :, :], ALU.mult))
            dve.reduce_sum(loop_count[:, :], wf_loop[:, :, :], AX.X)
            own_step(dve.tensor_tensor(wf_in[:, :, :], wf_in[:, :, :], wf_loop[:, :, :], ALU.subtract))
            own_step(dve.scalar_tensor_tensor(wf_key[:, :, :], wf_src[:, :, :], float(P), wf_rel[:, :, :],
                                              op0=ALU.mult, op1=ALU.add))
            own_step(dve.scalar_tensor_tensor(wf_key[:, :, :], wf_key[:, :, :], 1.0, wf_in[:, :, :],
                                              op0=ALU.add, op1=ALU.mult))
            own_step(dve.tensor_scalar(nodes_in[:, :], tile_base[:, :], -1.0, float(N_NODES), op0=ALU.mult, op1=ALU.add))
            own_step(dve.tensor_scalar(nodes_in[:, :], nodes_in[:, :], 0.0, float(P), op0=ALU.max, op1=ALU.min))
            own_step(dve.tensor_tensor(nodes_in[:, :], nodes_in[:, :], loop_count[:, :], ALU.not_equal))
            dve.reduce_sum(faults[0:TP, 2:3], nodes_in[:, :], AX.X)
            own_step(dve.tensor_scalar(below[:, :], wf_rel[:, :, WIN - 1], float(P), None, op0=ALU.is_lt))
            own_step(dve.reduce_sum(faults[0:TP, 3:4], below[:, :], AX.X))

            picked = done[0]
            with dve.Fori(0, P // 8) as r:
                for c in range(CHUNKS):
                    last = dve.max(top8[:, c, :], wf_key[:, c, :])
                last.then_inc(prep, 1)
                dve.wait_ge(prep, r * 2 + (picked + 1))
                dve.tensor_copy(keys[:, :, bass.ds(r * 8, 8)], top8[:, :, :])
                for c in range(CHUNKS):
                    last = dve.match_replace(wf_key[:, c, :], top8[:, c, :], wf_key[:, c, :], 0.0)
                last.then_inc(prep, 1)
                dve.wait_ge(prep, r * 2 + (picked + 2))
                dve.sem_inc(keys_ready, 1)
            done[0] += 2 * (P // 8)
            dve.reduce_max(faults[0:TP, 4:5], wf_key[:, :, :], AX.XY).then_inc(faults_ready, 1)
            dve.wait_ge(keys_turned, 1)
            own_step(dve.tensor_copy(keys_t[:, 0:4 * TP], ps["turn"][0][:, 0:4 * TP]))
            own_step(dve.tensor_copy(keys_t[:, 4 * TP:TILES], ps["turn"][1][:, 0:(CHUNKS - 4) * TP]))
            dve.tensor_scalar(key_i[:, :], keys_t[:, :], -1.0, None, op0=ALU.add)
            own_step(dve.tensor_scalar(empty_t[:, :], keys_t[:, :], 0.0, -float(SENTINEL), op0=ALU.is_equal,
                                       op1=ALU.mult))
            dve.tensor_scalar(slot_index[:, :], key_i[:, :], 7, None, op0=ALU.logical_shift_right)
            own_step(dve.tensor_scalar(node_i[:, :], key_i[:, :], P - 1, None, op0=ALU.bitwise_and))
            own_step(dve.tensor_tensor(slot_node[:, :], node_i[:, :], empty_t[:, :], ALU.add))
            dve.wait_ge(faults_summed, 1)
            own_step(dve.reduce_sum(fault_sum[:, :], ps["out"][0][:, 0:8], AX.X))
            dve.tensor_scalar(fast[:, :], fault_sum[:, :], 0.0, None, op0=ALU.is_equal)
            own_step(dve.tensor_scalar(general_flag[:, :], fault_sum[0:1, :], 0.0, None, op0=ALU.is_gt))
            dve.sem_inc(flag_set, 1)
            dve.sem_inc(tables_ready, 1)

            def norm_step(s):
                if s.live():
                    dve.wait_ge(x_loaded[s.slot], (s.use + 1) * 16)
                    for j in range(4):
                        last = dve.bn_stats(stats[s.half][:, j, :], xg[s.slot][:, j, :])
                    last.then_inc(stats_done, 1)
                t = s.back(1)
                if t.live():
                    dve.wait_ge(std_ready, t.n + 1)
                    if t.has(2):
                        dve.wait_ge(h0_ready, t.back(2).n + 1)
                    if s.live():
                        dve.wait_ge(stats_done, s.n + 1)
                    dve.reciprocal(rstd[t.half][:, :], std[t.half][:, :]).then_inc(recip_done, 1)
                if s.live():
                    if not t.live():
                        dve.wait_ge(stats_done, s.n + 1)
                    for j in range(4):
                        last = dve.bn_aggr(moments[s.half][:, j, :], stats[s.half][:, j, :])
                    last.then_inc(moments_ready, 1)
                if t.live():
                    dve.wait_ge(recip_done, t.n + 1)
                    dve.scalar_tensor_tensor(shift[t.half][:, :], moments[t.half][:, :, 0], -1.0, rstd[t.half][:, :],
                                             op0=ALU.mult, op1=ALU.mult).then_inc(norm_ready, 1)
            pipeline(dve, norm_step, GROUPS, 1)

            def general(pass_no):
                table, sums, width = GENERAL[pass_no]
                with dve.If(dve.value_load(general_flag[0:1, 0:1], min_val=0, max_val=1) != 0):
                    with_degree = pass_no == 0
                    first = pass_no * EW
                    if with_degree:
                        dve.wait_ge(ge_loaded, 16)
                        dve.tensor_scalar(ge_before[:, :], iota_row[0:EP, 0:EP], iota_col[0:EP, :], None,
                                          op0=ALU.is_lt)
                    steps = 6
                    own = [0]
                    with dve.Fori(0, EW) as i:
                        def mine(ins):
                            own[0] += 1
                            ins.then_inc(ge_dve, 1)
                            dve.wait_ge(ge_dve, i * steps + (first * steps + own[0]))
                        column = dst_all[:, bass.ds(i, 1)]
                        dve.tensor_copy(ge_src[:, :], src_all[:, bass.ds(i, 1)])
                        dve.tensor_copy(ge_at[:, :], column)
                        mine(dve.tensor_copy(ge_dst[:, :], column))
                        dve.tensor_scalar(ge_dst_b[:, :], iota_row[0:EP, 0:EP], 0.0, ge_dst[:, :], op0=ALU.mult,
                                          op1=ALU.add).then_inc(ge_spread, 1)
                        dve.wait_ge(ge_turned, i + (first + 1))
                        mine(dve.tensor_scalar(ge_same[:, :], ps["hid"][1][0:EP, 0:EP], ge_dst[:, :], None,
                                               op0=ALU.is_equal))
                        dve.reduce_sum(ge_count[:, :], ge_same[:, :], AX.X)
                        mine(dve.tensor_tensor(ge_mask[:, :], ge_same[:, :], ge_before[:, :], ALU.mult))
                        mine(dve.reduce_sum(ge_dup[:, :], ge_mask[:, :], AX.X))
                        mine(dve.tensor_scalar(ge_dup[:, :], ge_dup[:, :], 0.0, float(SENTINEL), op0=ALU.is_gt,
                                               op1=ALU.mult))
                        mine(dve.tensor_tensor(ge_put_at[:, :], ge_dst[:, :], ge_dup[:, :], ALU.add))
                        dve.sem_inc(ge_index, 1)
                        dve.wait_ge(ge_summed, i + (first + 1))
                        fetches = 3 if with_degree else 2
                        fetched = [0, 3, 5][pass_no] * EW
                        dve.wait_ge(ge_fetched, i * (16 * fetches) + 16 * (fetched + fetches))
                        if with_degree:
                            dve.tensor_tensor(ge_deg_new[:, :], ge_deg[:, :], ge_count[:, :], ALU.add)
                        dve.tensor_tensor(ge_new[:, 0:width], ps["hid"][0][0:EP, 0:width], ge_cur[:, 0:width],
                                          ALU.add).then_inc(ge_new_ready, 1)
                        puts = 2 if with_degree else 1
                        put = [0, 2, 3][pass_no] * EW
                        dve.wait_ge(ge_put, i * (16 * puts) + 16 * (put + puts))
                    if with_degree:
                        dve.wait_ge(ge_base_loaded, 16)
                        dve.tensor_scalar(base_degree[:, :], ge_base[:, :], 1.0, None, op0=ALU.max)
                        dve.tensor_scalar(slot_node[:, :], ge_base[:, :], 0.0, iota_col[:, :], op0=ALU.mult,
                                          op1=ALU.add).then_inc(ge_dve, 1)
                        dve.wait_ge(ge_dve, steps * EW + 1)
                    if with_degree:
                        dve.sem_inc(ge_tables, 1)
                    dve.sem_inc(ge_done, 1)

            def selects(layer, s):
                if not s.live():
                    return
                if s.has(2):
                    dve.wait_ge(layer.summed, s.back(2).n + 1)
                for j in range(2):
                    last = dve.tensor_scalar(select[s.half][:, j, :], iota_row[:, :],
                                             slot_node[:, bass.ds(s.n * 2 + j, 1)], None, op0=ALU.is_equal)
                last.then_inc(layer.selected, 1)

            def means(layer, s, width, stride):
                if not s.live():
                    return
                dve.wait_ge(layer.summed, s.n + 1)
                dve.wait_ge(layer.own_scaled, s.n + 1)
                if s.has(2):
                    dve.wait_ge(layer.turned, s.back(2).n + 1)
                for j in range(2):
                    last = dve.scalar_tensor_tensor(agg[s.half][:, j, 0:width],
                                                    ps["agg"][s.half][:, j * stride:j * stride + width],
                                                    inv_degree[:, bass.ds(s.n * 2 + j, 1)],
                                                    own_scaled[s.half][:, j, 0:width], op0=ALU.mult, op1=ALU.add)
                last.then_inc(layer.agg_ready, 1)

            general(0)

            def layer0(ahead):
                s = ahead.back(1)
                if s.live():
                    dve.wait_ge(L0.summed, s.n + 1)
                    two = bass.ds(s.n * 2, 2)
                    counts = ps["agg"][s.half][:, :].rearrange("p (j f) -> p j f", j=2)[:, :, D]
                    dve.scalar_tensor_tensor(degree[s.half][:, :], counts, fast[:, :], base_degree[:, two],
                                             op0=ALU.mult, op1=ALU.add).then_inc(L0.degree_done, 1)
                selects(L0, ahead)
                if s.live():
                    dve.wait_ge(L0.degree_done, s.n + 1)
                    dve.reciprocal(inv_degree[:, two], degree[s.half][:, :]).then_inc(L0.recip_done, 1)
                    dve.wait_ge(L0.recip_done, s.n + 1)
                    dve.tensor_scalar(self_scale[:, two], inv_degree[:, two], fast[:, :], None, op0=ALU.mult
                                      ).then_inc(L0.scale_ready, 1)
                t = s.back(1)
                if t.live():
                    dve.wait_ge(L0.turned, t.n + 1)
                    if t.has(2):
                        dve.wait_ge(L0.dense_done, t.back(2).n + 1)
                    dve.tensor_copy(cat_t[t.half][:, 0:2, :], ps["turn"][t.half][:, :].rearrange("p (k n) -> p k n", k=2)
                                    ).then_inc(L0.cat_ready, 1)
                means(L0, s, D, H)
            pipeline(dve, layer0, PAIRS, 2)

            general(1)

            def layer1(ahead):
                s = ahead.back(1)
                selects(L1, ahead)
                means(L1, s, H, H)
                t = s.back(1)
                if t.live():
                    dve.wait_ge(L1.turned, t.n + 1)
                    if t.has(2):
                        dve.wait_ge(L1.hid_done, t.back(2).n + 1)
                    dve.tensor_copy(cat_t[t.half][:, :, 0:P], ps["turn"][0][:, :].rearrange("p (k n) -> p k n", k=4)
                                    ).then_inc(L1.cat_ready, 1)
                t = s.back(3)
                if t.live():
                    dve.wait_ge(L1.dense_done, t.n + 1)
                    dve.wait_ge(L1.z_ready, t.n + 1)
                    for j in range(2):
                        last = dve.scalar_tensor_tensor(y_mid[t.half][:, j, :], z_out[t.slot][:, j, :],
                                                        self_scale[:, bass.ds(t.n * 2 + j, 1)],
                                                        ps["out"][t.half][:, j * H + D:(j + 1) * H],
                                                        op0=ALU.mult, op1=ALU.add)
                    last.then_inc(L1.y_mid_ready, 1)
                    dve.wait_ge(L1.y_mid_ready, t.n + 1)
                    dve.wait_ge(L1.x_loaded[t.slot], (t.use + 1) * 16)
                    if t.has(SLOTS):
                        dve.wait_ge(L1.stored[t.slot], t.use * 32)
                    dve.tensor_tensor(y_out[t.slot][:, :, :], y_mid[t.half][:, :, :], x_in[t.slot][:, :, :], ALU.add
                                      ).then_inc(L1.rows_ready, 1)
            pipeline(dve, layer1, PAIRS, 4)

            general(2)

            def layer2(ahead):
                s = ahead.back(1)
                selects(L2, ahead)
                if s.live():
                    dve.wait_ge(L2.own_loaded[s.slot], (s.use + 1) * 16)
                    dve.wait_ge(L2.summed, s.n + 1)
                    if s.has(SLOTS):
                        dve.wait_ge(L2.stored[s.slot], s.use * 16)
                    for j in range(2):
                        last = dve.scalar_tensor_tensor(y_out[s.slot][:, j, :], ps["agg"][s.half][:, j * H:j * H + D],
                                                        inv_degree[:, bass.ds(s.n * 2 + j, 1)],
                                                        own[s.slot][:, j, 0:D], op0=ALU.mult, op1=ALU.add)
                    last.then_inc(L2.rows_ready, 1)
            pipeline(dve, layer2, PAIRS, 1)

        @block.tensor
        def _(pe):
            pe.wait_ge(const_made, 2)
            pe.wait_ge(keys_ready, P // 8)
            for c in range(CHUNKS):
                at = (c % 4) * TP
                last = nc.tensor.matmul(ps["turn"][c // 4][:, at:at + TP], keys[:, c, :], ident[0:TP, 0:TP],
                                        is_transpose=True, start=True, stop=True)
            last.then_inc(keys_turned, 1)
            pe.wait_ge(faults_ready, 1)
            nc.tensor.matmul(ps["out"][0][:, 0:8], ones[:, :], faults[:, :], start=True, stop=True
                             ).then_inc(faults_summed, 1)

            def general(pass_no):
                table, sums, width = GENERAL[pass_no]
                with pe.If(pe.value_load(general_flag[0:1, 0:1], min_val=0, max_val=1) != 0):
                    with_degree = pass_no == 0
                    fetches = 3 if with_degree else 2
                    fetched = [0, 3, 5][pass_no] * EW
                    first = pass_no * EW
                    with pe.Fori(0, EW) as i:
                        pe.wait_ge(ge_spread, i + (first + 1))
                        nc.tensor.matmul(ps["hid"][1][0:EP, 0:EP], ge_dst_b[:, :], ident[0:EP, 0:EP],
                                         is_transpose=True, start=True, stop=True).then_inc(ge_turned, 1)
                        pe.wait_ge(ge_index, i + (first + 1))
                        pe.wait_ge(ge_fetched, i * (16 * fetches) + 16 * (fetched + fetches))
                        nc.tensor.matmul(ps["hid"][0][0:EP, 0:width], ge_same[:, :], ge_msg[:, 0:width],
                                         start=True, stop=True).then_inc(ge_summed, 1)
                    pe.wait_ge(ge_new_ready, first + EW)

            def sums(layer, s, width, stride):
                if not s.live():
                    return
                pe.wait_ge(layer.gathered[s.slot], (s.use + 1) * 32)
                pe.wait_ge(layer.selected, s.n + 1)
                if s.has(2):
                    pe.wait_ge(layer.rows_ready if layer is L2 else layer.agg_ready, s.back(2).n + 1)
                for j in range(2):
                    last = nc.tensor.matmul(ps["agg"][s.half][:, j * stride:j * stride + width],
                                            select[s.half][:, j, :], nbr[s.slot][:, j, 0:width],
                                            start=True, stop=True)
                last.then_inc(layer.summed, 1)

            pe.wait_ge(w_loaded, 16 * 9)
            pe.wait_ge(bias_moved, 16 * 3)
            pe.wait_ge(flag_set, 1)
            general(0)

            def layer0(s):
                sums(L0, s, D + 1, H)
                t = s.back(2)
                if t.live():
                    pe.wait_ge(L0.cat_ready, t.n + 1)
                    if t.has(2):
                        pe.wait_ge(L0.rows_ready, t.back(2).n + 1)
                    for j in range(2):
                        o = ps["out"][t.half][:, j * H:(j + 1) * H]
                        nodes = slice(j * P, (j + 1) * P)
                        nc.tensor.matmul(o, ones3[:, :], bias3[:, 0:H], start=True, stop=False)
                        nc.tensor.matmul(o, cat_t[t.half][:, 0, nodes], w0[:, 0, :], start=False, stop=False)
                        last = nc.tensor.matmul(o, cat_t[t.half][:, 1, nodes], w0[:, 1, :], start=False, stop=True)
                    last.then_inc(L0.dense_done, 1)
                t = s.back(1)
                if t.live():
                    pe.wait_ge(L0.agg_ready, t.n + 1)
                    pe.wait_ge(L0.own_loaded[t.slot], (t.use + 1) * 16)
                    if t.has(2):
                        pe.wait_ge(L0.cat_ready, t.back(2).n + 1)
                    for j in range(2):
                        for k, rows in enumerate((own[t.slot], agg[t.half])):
                            at = k * PAIR + j * P
                            last = nc.tensor.matmul(ps["turn"][t.half][:, at:at + P], rows[:, j, 0:D], ident[:, :],
                                                    is_transpose=True, start=True, stop=True)
                    last.then_inc(L0.turned, 1)
            pipeline(pe, layer0, PAIRS, 2)

            general(1)

            def layer1(s):
                sums(L1, s, H, H)
                t = s.back(1)
                if t.live():
                    pe.wait_ge(L1.agg_ready, t.n + 1)
                    pe.wait_ge(L1.own_loaded[t.slot], (t.use + 1) * 16)
                    if t.has(1):
                        pe.wait_ge(L1.cat_ready, t.back(1).n + 1)
                        pe.wait_ge(L1.cat_ready_act, t.back(1).n + 1)
                    for j in range(2):
                        for k in range(4):
                            rows = (own[t.slot], agg[t.half])[k // 2][:, j, (k % 2) * P:(k % 2 + 1) * P]
                            last = nc.tensor.matmul(ps["turn"][j][:, k * P:(k + 1) * P], rows, ident[:, :],
                                                    is_transpose=True, start=True, stop=True)
                    last.then_inc(L1.turned, 1)
                t = s.back(2)
                if t.live():
                    pe.wait_ge(L1.cat_ready, t.n + 1)
                    pe.wait_ge(L1.cat_ready_act, t.n + 1)
                    if t.has(2):
                        pe.wait_ge(L1.h2_ready, t.back(2).n + 1)
                    for m in range(2):
                        for k in range(4):
                            last = nc.tensor.matmul(ps["hid"][t.half][:, m * PAIR:(m + 1) * PAIR],
                                                    w1[:, k, m * P:(m + 1) * P], cat_t[t.half][:, k, :],
                                                    start=k == 0, stop=k == 3)
                    last.then_inc(L1.hid_done, 1)
                t = s.back(3)
                if t.live():
                    pe.wait_ge(L1.h2_ready, t.n + 1)
                    if t.has(2):
                        pe.wait_ge(L1.rows_ready, t.back(2).n + 1)
                    for j in range(2):
                        o = ps["out"][t.half][:, j * H:(j + 1) * H]
                        nodes = slice(j * P, (j + 1) * P)
                        nc.tensor.matmul(o, h2_t[t.half][:, 0, nodes], w2[:, 0, :], start=True, stop=False)
                        nc.tensor.matmul(o, h2_t[t.half][:, 1, nodes], w2[:, 1, :], start=False, stop=False)
                        last = nc.tensor.matmul(o[:, D:2 * D], ones3[:, :], bias3[:, H:H + D], start=False, stop=True)
                    last.then_inc(L1.dense_done, 1)
            pipeline(pe, layer1, PAIRS, 3)

            general(2)
            pipeline(pe, lambda s: sums(L2, s, D, H), PAIRS, 0)


INPUTS = ["x", "src", "dst", "L0_gnn_ws0", "L0_gnn_wn0", "L0_gnn_b0", "L0_gnn_ws1", "L0_gnn_wn1", "L0_gnn_b1",
          "L0_gnn_ws2", "L0_gnn_wn2", "L0_gnn_b2"]


def kernel(**inputs):
    import numpy as np
    import concourse.bacc as bacc
    from concourse.bass_utils import run_bass_kernel_spmd

    nc = bacc.Bacc("TRN2", target_bir_lowering=False, num_devices=1)
    arrays, args = {}, []
    for name in INPUTS:
        a = np.ascontiguousarray(inputs[name])
        if name == "x":
            padded = np.zeros((N_PAD, D), a.dtype)
            padded[:N_NODES] = a
            a = padded
        arrays[f"in_{name}"] = a
        args.append(nc.dram_tensor(f"in_{name}", a.shape, mybir.dt.from_np(a.dtype), kind="ExternalInput").ap())
    out = nc.dram_tensor("out_rows", (N_PAD, D), FP32, kind="ExternalOutput").ap()
    build(nc, *args, out)
    r = run_bass_kernel_spmd(nc, [arrays], core_ids=[0])
    return r.results[0]["out_rows"][:N_NODES]
```

```python
import concourse.bass as bass
from concourse import mybir
from contextlib import ExitStack

FP32 = mybir.dt.float32
FP32R = mybir.dt.float32r
BF16 = mybir.dt.bfloat16
I32 = mybir.dt.int32
ALU = mybir.AluOpType
ACT = mybir.ActivationFunctionType
AX = mybir.AxisListType

P = 128
N_NODES = 100000
N_EDGES = 150000
D = 128
H = 256
PAIR = 2 * P
SLOTS = 4
PAIRS = -(-N_NODES // (PAIR * SLOTS)) * SLOTS
TILES = 2 * PAIRS
N_PAD = TILES * P
GROUP = 4 * P
GROUPS = N_PAD // GROUP
CHUNKS = 7
TP = TILES // CHUNKS
ROW = 120
ROWS = N_EDGES // ROW
WROWS = 3
WIN = WROWS * ROW
EP = 125
EW = N_EDGES // EP
SENTINEL = 1 << 20
EPS = 1e-5
NORM_SLOTS = 7
NORM_BEFORE_KEYS = 3
NORM_AFTER_KEYS = NORM_BEFORE_KEYS + P // 8
LAYER_MEM = 5 * CHUNKS * WIN


class Step:

    def __init__(self, use, slot, total, looped, slots):
        self.use, self.slot, self.total, self.looped, self.slots = use, slot, total, looped, slots
        self.n = use * slots + slot if not looped or slot else use * slots
        self.half = slot % 2

    def back(self, lag):
        at = self.slot - lag
        rounds = at // self.slots
        return Step(self.use + rounds if rounds else self.use, at % self.slots, self.total, self.looped, self.slots)

    def live(self):
        return self.looped or 0 <= self.n < self.total

    def has(self, earlier):
        return self.looped or self.n >= earlier


def peeled(step, first, last, total, slots=SLOTS):
    for n in range(first, last):
        step(Step(n // slots, n % slots, total, False, slots))


def looped(eng, step, first_use, last_use, total, slots=SLOTS):
    with eng.Fori(first_use, last_use) as i:
        for slot in range(slots):
            step(Step(i, slot, total, True, slots))


def pipeline(eng, step, total, lag, rounds=2, slots=SLOTS):
    assert lag < rounds * slots and total % slots == 0
    peeled(step, 0, rounds * slots, total, slots)
    looped(eng, step, rounds, total // slots, total, slots)
    peeled(step, total, total + lag, total, slots)


def build(nc, x, src, dst, ws0, wn0, b0, ws1, wn1, b1, ws2, wn2, b2, out):
    h0_dram = nc.dram_tensor("h0_rows", [N_PAD, D], FP32).ap()
    h1_dram = nc.dram_tensor("h1_rows", [N_PAD, H], FP32).ap()
    z_dram = nc.dram_tensor("z_rows", [N_PAD, D], FP32).ap()
    h0_sums = nc.dram_tensor("h0_sums", [N_PAD, D], FP32).ap()
    h1_sums = nc.dram_tensor("h1_sums", [N_PAD, H], FP32).ap()
    z_sums = nc.dram_tensor("z_sums", [N_PAD, D], FP32).ap()
    y_dram = nc.dram_tensor("y_rows", [N_PAD, D], FP32).ap()
    samples_dram = nc.dram_tensor("dst_samples", [EP, EW // ROW], FP32).ap()
    degree_dram = nc.dram_tensor("general_degrees", [N_PAD, 1], FP32).ap()

    src_rows = src.rearrange("(r w) -> r w", w=ROW)
    dst_rows = dst.rearrange("(r w) -> r w", w=ROW)
    src_flat = src.rearrange("(p w) -> p w", w=EW)
    dst_flat = dst.rearrange("(p w) -> p w", w=EW)

    with ExitStack() as ctx:
        def sb(name, shape, dt=FP32):
            return ctx.enter_context(nc.sbuf_tensor(name, shape, dt))

        def sem(name):
            return ctx.enter_context(nc.semaphore(name))

        def sems(name, n=SLOTS):
            return [sem(f"{name}{i}") for i in range(n)]

        iota_row = sb("iota_row", [P, P])
        iota_col = sb("iota_col", [P, 1])
        iota_row_i = sb("iota_row_i", [P, P], I32)
        iota_col_i = sb("iota_col_i", [P, 1], I32)
        ident = sb("ident", [P, P])
        ones = sb("ones", [P, P])
        ones3 = sb("ones3", [3, P], BF16)
        eps_col = sb("eps_col", [P, 1])
        w_hi = sb("w_hi", [P, 8, H], FP32R)
        w_lo = sb("w_lo", [P, 8, H], FP32R)
        W0, W1, W2 = 0, 2, 6
        b1_col = sb("b1_col", [P, 2])
        bias_row = sb("bias_row", [1, H + D])
        bias_rest = sb("bias_rest", [1, 2, H + D])
        bias_part = sb("bias_part", [1, 3, H + D], BF16)
        bias3 = sb("bias3", [3, H + D], BF16)

        slot_index = sb("slot_index", [P, TILES], I32)
        slot_node = sb("slot_node", [P, TILES])
        base_degree = sb("base_degree", [P, TILES])
        inv_degree = sb("inv_degree", [P, TILES])
        self_scale = sb("self_scale", [P, TILES])
        fast = sb("fast", [P, 1])
        general_flag = sb("general_flag", [1, 1], I32)

        layer_mem = sb("layer_mem", [P, LAYER_MEM])
        taken = [0]

        def part(a, b):
            at = taken[0]
            taken[0] += a * b
            assert taken[0] <= LAYER_MEM
            return layer_mem[:, at:at + a * b].rearrange("p (a b) -> p a b", a=a)

        weights = layer_mem[:, 0:8 * H].rearrange("p (k n) -> p k n", k=8)

        dst_all = sb("dst_all", [EP, EW], I32)
        dst_next = sb("dst_next", [EP - 1, 2], I32)
        samples = sb("samples", [EP, EW // ROW])
        samples_b = sb("samples_b", [TP, ROWS])
        scratch_rows = sb("scratch_rows", [P, ROWS])
        tile_base_i = sb("tile_base_i", [TP, CHUNKS], I32)
        tile_base = sb("tile_base", [TP, CHUNKS])
        below = sb("below", [TP, CHUNKS])
        row_f = sb("row_f", [TP, CHUNKS])
        row_index = sb("row_index", [TP, WROWS, CHUNKS], I32)
        win_dst = sb("win_dst", [TP, CHUNKS, WIN], I32)
        win_src_mem = sb("win_src_mem", [P, CHUNKS * WIN], I32)
        win_src = win_src_mem[0:TP, :].rearrange("p (c w) -> p c w", c=CHUNKS)
        wf_dst, wf_src, wf_rel, wf_in, wf_loop = (
            layer_mem[0:TP, i * CHUNKS * WIN:(i + 1) * CHUNKS * WIN].rearrange("p (c w) -> p c w", c=CHUNKS)
            for i in range(5))
        wf_key_mem = sb("wf_key_mem", [P, CHUNKS * WIN])
        wf_key = wf_key_mem[0:TP, :].rearrange("p (c w) -> p c w", c=CHUNKS)
        loop_count = sb("loop_count", [TP, CHUNKS])
        nodes_in = sb("nodes_in", [TP, CHUNKS])
        top8 = sb("top8", [TP, CHUNKS, 8])
        keys = sb("keys", [TP, CHUNKS, P])
        keys_t = sb("keys_t", [P, TILES])
        empty_t = sb("empty_t", [P, TILES])
        key_i = sb("key_i", [P, TILES], I32)
        node_i = sb("node_i", [P, TILES], I32)
        faults = sb("faults", [P, 8])
        fault_sum = sb("fault_sum", [P, 1])

        loaded_rows = [sb(f"loaded_rows{i}", [P, 2 * H]) for i in range(SLOTS)]
        stored_rows = [sb(f"stored_rows{i}", [P, 2 * H]) for i in range(SLOTS)]
        norm_rows = [t[:, :].rearrange("p (j f) -> p j f", j=4) for t in (loaded_rows + stored_rows)[:NORM_SLOTS]]
        stats = [sb(f"stats{i}", [P, 4, 6]) for i in range(NORM_SLOTS)]
        moments = [sb(f"moments{i}", [P, 4, 2]) for i in range(NORM_SLOTS)]
        std = [sb(f"std{i}", [P, 4]) for i in range(NORM_SLOTS)]
        rstd = [sb(f"rstd{i}", [P, 4]) for i in range(NORM_SLOTS)]
        shift = [sb(f"shift{i}", [P, 4]) for i in range(NORM_SLOTS)]

        own = [t[:, :].rearrange("p (j f) -> p j f", j=2) for t in loaded_rows]
        nbr = [part(2, H) for i in range(SLOTS)]
        nbr_hi = [sb(f"nbr_hi{i}", [P, 2, H], FP32R) for i in range(2)]
        nbr_lo = [sb(f"nbr_lo{i}", [P, 2, H], FP32R) for i in range(2)]
        gather_at = [sb(f"gather_at{i}", [P, 2], I32) for i in range(SLOTS)]
        select = [sb(f"select{i}", [P, 2, P], FP32R) for i in range(2)]
        degree = [sb(f"degree{i}", [P, 2]) for i in range(2)]
        own_scaled = [part(2, H) for i in range(2)]
        agg = [part(2, H) for i in range(2)]
        cat_hi = [sb(f"cat_hi{i}", [P, 4, PAIR], FP32R) for i in range(2)]
        cat_lo = [sb(f"cat_lo{i}", [P, 4, PAIR], FP32R) for i in range(2)]
        h2 = [part(2, PAIR) for i in range(2)]
        h2_hi = [sb(f"h2_hi{i}", [P, 2, PAIR], FP32R) for i in range(2)]
        h2_lo = [sb(f"h2_lo{i}", [P, 2, PAIR], FP32R) for i in range(2)]
        h1_out = [t[:, :].rearrange("p (j f) -> p j f", j=2) for t in stored_rows]
        z_out = [part(2, D) for i in range(SLOTS)]
        y_mid = [part(2, D) for i in range(2)]
        y_out = [part(2, D) for i in range(SLOTS)]
        x_in = [part(2, D) for i in range(SLOTS)]

        src_all = win_src_mem[0:EP, 0:EW]
        ge_base = keys_t
        ge_taken = [0]

        def ge_part(rows, width):
            at = ge_taken[0]
            ge_taken[0] += width
            assert ge_taken[0] <= CHUNKS * WIN
            return wf_key_mem[0:rows, at:at + width]

        zero_rows = ge_part(P, 4 * H)
        ge_dst_b = ge_part(EP, EP)
        ge_same = ge_part(EP, EP)
        ge_before = ge_part(EP, EP)
        ge_mask = ge_part(EP, EP)
        ge_msg = ge_part(EP, H)
        ge_cur = ge_part(EP, H)
        ge_new = ge_part(EP, H)
        ge_src = sb("ge_src", [EP, 1], I32)
        ge_at = sb("ge_at", [EP, 1], I32)
        ge_put_at = sb("ge_put_at", [EP, 1], I32)
        ge_dst = sb("ge_dst", [EP, 1])
        ge_dup = sb("ge_dup", [EP, 1])
        ge_count = sb("ge_count", [EP, 1])
        ge_deg = sb("ge_deg", [EP, 1])
        ge_deg_new = sb("ge_deg_new", [EP, 1])

        ps = {k: [ctx.enter_context(nc.psum_tensor(f"ps_{k}{i}", [P, 512], FP32)) for i in range(2)]
              for k in ("agg", "turn", "hid", "out")}

        w_loaded, bias_moved = sem("w_loaded"), sem("bias_moved")
        iota_made, const_made = sem("iota_made"), sem("const_made")
        bias_split, w_hi_ready, w_ready = sem("bias_split"), sem("w_hi_ready"), sem("w_ready")
        dst_loaded, sampled, sample_stored, sample_spread = (
            sem("dst_loaded"), sem("sampled"), sem("sample_stored"), sem("sample_spread"))
        rows_found, win_cleared, win_gathered = sem("rows_found"), sem("win_cleared"), sem("win_gathered")
        prep = sem("prep")
        keys_ready, keys_turned = sem("keys_ready"), sem("keys_turned")
        faults_ready, faults_summed, flag_set = sem("faults_ready"), sem("faults_summed"), sem("flag_set")
        tables_ready = sem("tables_ready")
        nbr_cleared = sem("nbr_cleared")

        x_loaded, stats_done, moments_ready = sems("x_loaded", NORM_SLOTS), sem("stats_done"), sem("moments_ready")
        std_ready, recip_done, norm_ready = sem("std_ready"), sem("recip_done"), sem("norm_ready")
        h0_ready, h0_stored = sem("h0_ready"), sems("h0_stored", NORM_SLOTS)

        class Layer:

            def __init__(self, n):
                self.own_loaded = sems(f"own_loaded_{n}_")
                self.index_copied = sem(f"index_copied_{n}")
                self.gathered = sems(f"gathered_{n}_")
                self.selected = sem(f"selected_{n}")
                self.summed = sem(f"summed_{n}")
                self.rows_ready = sem(f"rows_ready_{n}")
                self.stored = sems(f"stored_{n}_")
                if n < 2:
                    self.own_scaled = sem(f"own_scaled_{n}_done")
                    self.agg_ready = sem(f"agg_ready_{n}")
                    self.turned = sem(f"turned_{n}")
                    self.cat_hi_ready = sem(f"cat_hi_ready_{n}")
                    self.cat_ready = sem(f"cat_ready_{n}")
                    self.dense_done = sem(f"dense_done_{n}")
                if n == 0:
                    self.degree_done = sem("degree_done")
                    self.recip_done = sem("inv_degree_done")
                    self.scale_ready = sem("scale_ready")
                if n == 1:
                    self.nbr_hi_ready = sem("nbr_hi_ready")
                    self.nbr_split = sem("nbr_split")
                    self.x_loaded = sems("x_in_loaded")
                    self.hid_done = sem("hid_done")
                    self.h2_made = sem("h2_made")
                    self.h2_hi_ready = sem("h2_hi_ready")
                    self.h2_lo_ready = sem("h2_lo_ready")
                    self.z_ready = sem("z_ready")
                    self.y_mid_ready = sem("y_mid_ready")

        sp_may_load = sem("sp_may_load")
        pool_may_go = sem("pool_may_go")

        L0, L1, L2 = Layer(0), Layer(1), Layer(2)

        ge_loaded, ge_zeroed = sem("ge_loaded"), sem("ge_zeroed")
        ge_dve, ge_spread, ge_turned, ge_index = sem("ge_dve"), sem("ge_spread"), sem("ge_turned"), sem("ge_index")
        ge_fetched, ge_summed, ge_new_ready, ge_put = (
            sems("ge_fetched", 3), sem("ge_summed"), sem("ge_new_ready"), sems("ge_put", 3))
        ge_zero_made, ge_base_loaded, ge_index_set = sem("ge_zero_made"), sem("ge_base_loaded"), sem("ge_index_set")
        ge_cleared = sem("ge_cleared")
        ge_nodes_set = sem("ge_nodes_set")

        def pair_rows(table, s):
            return table[bass.ds(s.n * PAIR, PAIR), :].rearrange("(j p) f -> p j f", p=P)

        def group_rows(table, s):
            return table[bass.ds(s.n * GROUP, GROUP), :].rearrange("(p j) f -> p j f", p=P)

        def sum_bank(layer, s):
            return (ps["agg"] + ps["hid"])[s.slot if layer is L0 else s.half][:, :]

        def all_stored(eng, stored, per_slot):
            for one in stored:
                eng.wait_ge(one, per_slot * 16)

        SLOT_USES = PAIRS // SLOTS
        GENERAL = [(h0_dram, h0_sums, D), (h1_dram, h1_sums, H), (z_dram, z_sums, D)]
        ZERO_ROWS = 4 * P

        block = ctx.enter_context(nc.Block())

        @block.sync
        def _(sp):
            sp.dma_start(dst_all[:, :], dst_flat).then_inc(dst_loaded, 16)
            sp.dma_start(dst_next[:, :], dst_flat[1:EP, 0:2]).then_inc(dst_loaded, 16)
            sp.dma_start(bias_row[:, 0:H], b0.rearrange("(a n) -> a n", a=1)).then_inc(w_loaded, 16)
            sp.dma_start(bias_row[:, H:H + D], b2.rearrange("(a n) -> a n", a=1)).then_inc(w_loaded, 16)
            sp.dma_start(b1_col[:, :], b1.rearrange("(m p) -> p m", p=P), allow_slow_non_contiguous=True).then_inc(w_loaded, 16)
            sp.dma_start(weights[:, W0, :], ws0).then_inc(w_loaded, 16)
            sp.dma_start(weights[:, W0 + 1, :], wn0).then_inc(w_loaded, 16)
            sp.dma_start(weights[:, W1:W1 + 2, :], ws1.rearrange("(k p) n -> p k n", p=P)).then_inc(w_loaded, 16)
            sp.dma_start(weights[:, W1 + 2:W1 + 4, :], wn1.rearrange("(k p) n -> p k n", p=P)).then_inc(w_loaded, 16)
            sp.dma_start(weights[:, W2:W2 + 2, 0:D], wn2.rearrange("(k p) n -> p k n", p=P)).then_inc(w_loaded, 16)
            sp.dma_start(weights[:, W2:W2 + 2, D:2 * D], ws2.rearrange("(k p) n -> p k n", p=P)).then_inc(w_loaded, 16)
            sp.wait_ge(sampled, 1)
            sp.dma_start(samples_dram, samples[:, :]).then_inc(sample_stored, 16)
            sp.wait_ge(sample_stored, 16)
            sp.dma_start(samples_b[:, :], samples_dram.rearrange("(a p) w -> a (p w)", a=1).to_broadcast([TP, ROWS])
                         ).then_inc(sample_spread, 16)
            sp.wait_ge(bias_split, 5)
            for part in range(3):
                sp.dma_start(bias3[part:part + 1, :], bias_part[:, part, :]).then_inc(bias_moved, 16)

            def load_x(s):
                if not s.live():
                    return
                if s.has(NORM_SLOTS):
                    sp.wait_ge(h0_stored[s.slot], s.use * 16)
                    sp.sem_inc(sp_may_load, 1)
                sp.dma_start(norm_rows[s.slot][:, :, :], group_rows(x, s)).then_inc(x_loaded[s.slot], 16)
            pipeline(sp, load_x, GROUPS, 0, slots=NORM_SLOTS)

            def general(pass_no):
                table, sums, width = GENERAL[pass_no]
                with sp.If(sp.value_load(general_flag[0:1, 0:1], min_val=0, max_val=1) != 0):
                    if pass_no == 0:
                        sp.dma_start(src_all[:, :], src_flat).then_inc(ge_loaded, 16)
                        sp.wait_ge(ge_zero_made, 1)
                        sp.dma_start(degree_dram.rearrange("(a p c) o -> a p (c o)", a=1, p=P)[0],
                                     zero_rows[:, 0:TILES]).then_inc(ge_zeroed, 16)
                        sp.wait_ge(ge_zeroed, 16)
                    done = [1, 1 + GROUPS, 1 + 2 * GROUPS][pass_no]
                    with sp.Fori(0, GROUPS) as i:
                        sp.dma_start(sums[bass.ds(i * ZERO_ROWS, ZERO_ROWS), :]
                                     .rearrange("(p j) f -> p (j f)", p=P),
                                     zero_rows[:, 0:4 * width]).then_inc(ge_zeroed, 16)
                        sp.wait_ge(ge_zeroed, i * 16 + (done + 1) * 16)
                        sp.sem_inc(sp_may_load, 1)
                    sp.sem_inc(ge_cleared, 1)
                    if pass_no == 0:
                        sp.wait_ge(ge_put[0], 16 * 2 * EW)
                        sp.dma_start(ge_base[:, :], degree_dram.rearrange("(t p) o -> p (t o)", p=P),
                                     allow_slow_non_contiguous=True
                                     ).then_inc(ge_base_loaded, 16)

            def load_own(layer, table, width, s, freed):
                if not s.live():
                    return
                if s.has(SLOTS):
                    sp.wait_ge(freed, s.back(SLOTS).n + 1)
                    sp.sem_inc(sp_may_load, 1)
                sp.dma_start(own[s.slot][:, :, 0:width], pair_rows(table, s)).then_inc(layer.own_loaded[s.slot], 16)

            sp.wait_ge(flag_set, 1)
            all_stored(sp, h0_stored, GROUPS // NORM_SLOTS)
            general(0)
            pipeline(sp, lambda s: load_own(L0, h0_dram, D, s, L0.turned), PAIRS, 0)

            all_stored(sp, L0.stored, SLOT_USES)
            general(1)

            def layer1_loads(s):
                load_own(L1, h1_dram, H, s, L1.turned)
                t = s.back(4)
                if t.live():
                    if t.has(SLOTS):
                        sp.wait_ge(L1.rows_ready, t.back(SLOTS).n + 1)
                        sp.sem_inc(sp_may_load, 1)
                    sp.dma_start(x_in[t.slot][:, :, :], pair_rows(x, t)).then_inc(L1.x_loaded[t.slot], 16)
            pipeline(sp, layer1_loads, PAIRS, 4)

            all_stored(sp, L1.stored, 2 * SLOT_USES)
            general(2)
            pipeline(sp, lambda s: load_own(L2, y_dram, D, s, L2.rows_ready), PAIRS, 0)
            all_stored(sp, L2.stored, SLOT_USES)

        @block.gpsimd
        def _(pool):
            pool.iota(iota_row_i[:, :], pattern=[[1, P]], base=0, channel_multiplier=0).then_inc(iota_made, 1)
            pool.iota(iota_col_i[:, :], pattern=[[0, 1]], base=0, channel_multiplier=1).then_inc(iota_made, 1)
            pool.iota(tile_base_i[:, :], pattern=[[P * TP, CHUNKS]], base=0, channel_multiplier=P
                      ).then_inc(iota_made, 1)
            pool.memset(win_dst[:, :, :], SENTINEL).then_inc(win_cleared, 1)
            pool.memset(win_src[:, :, :], 0).then_inc(win_cleared, 1)
            pool.wait_ge(win_cleared, 2)
            pool.wait_ge(rows_found, 1)
            for c in range(CHUNKS):
                for r in range(WROWS):
                    for rows, win in ((dst_rows, win_dst), (src_rows, win_src)):
                        pool.indirect_dma_start(win[:, c, r * ROW:(r + 1) * ROW], None, rows,
                                                bass.IndirectOffsetOnAxis(row_index[:, r, c:c + 1], axis=0),
                                                bounds_check=ROWS - 1, oob_is_err=False).then_inc(win_gathered, 16)

            limit = pool.alloc_register("last_row")
            pool.reg_mov(limit, N_PAD - 1)
            last_row = pool.snap(limit)

            def general(pass_no):
                table, sums, width = GENERAL[pass_no]
                with pool.If(pool.value_load(general_flag[0:1, 0:1], min_val=0, max_val=1) != 0):
                    if pass_no == 0:
                        pool.memset(zero_rows[:, :], 0.0).then_inc(ge_zero_made, 1)
                        pool.iota(slot_index[:, :], pattern=[[P, TILES]], base=0, channel_multiplier=1
                                  ).then_inc(ge_index_set, 1)
                    pool.wait_ge(ge_cleared, pass_no + 1)
                    with_degree = pass_no == 0
                    puts = 2 if with_degree else 1
                    with pool.Fori(0, EW) as i:
                        pool.wait_ge(ge_index, i + (pass_no * EW + 1))
                        pool.sem_inc(pool_may_go, 1)
                        pool.indirect_dma_start(ge_msg[:, 0:width], None, table,
                                                bass.IndirectOffsetOnAxis(ge_src[:, :], axis=0),
                                                bounds_check=last_row, oob_is_err=False).then_inc(ge_fetched[pass_no], 16)
                        pool.indirect_dma_start(ge_cur[:, 0:width], None, sums,
                                                bass.IndirectOffsetOnAxis(ge_at[:, :], axis=0),
                                                bounds_check=last_row, oob_is_err=False).then_inc(ge_fetched[pass_no], 16)
                        if with_degree:
                            pool.indirect_dma_start(ge_deg[:, :], None, degree_dram,
                                                    bass.IndirectOffsetOnAxis(ge_at[:, :], axis=0),
                                                    bounds_check=N_PAD - 1, oob_is_err=False
                                                    ).then_inc(ge_fetched[pass_no], 16)
                        pool.wait_ge(ge_new_ready, i + (pass_no * EW + 1))
                        pool.sem_inc(pool_may_go, 1)
                        pool.indirect_dma_start(sums, bass.IndirectOffsetOnAxis(ge_put_at[:, :], axis=0),
                                                ge_new[:, 0:width], None,
                                                bounds_check=last_row, oob_is_err=False).then_inc(ge_put[pass_no], 16)
                        if with_degree:
                            pool.indirect_dma_start(degree_dram, bass.IndirectOffsetOnAxis(ge_put_at[:, :], axis=0),
                                                    ge_deg_new[:, :], None,
                                                    bounds_check=N_PAD - 1, oob_is_err=False).then_inc(ge_put[pass_no], 16)
                        pool.wait_ge(ge_put[pass_no], i * (16 * puts) + 16 * puts)
                        pool.sem_inc(pool_may_go, 1)
                    if pass_no == 0:
                        pool.wait_ge(ge_index_set, 1)

            def gathers(layer, table, width):
                def gather(s):
                    if not s.live():
                        return
                    if s.has(SLOTS):
                        pool.wait_ge(L1.nbr_split if layer is L1 else layer.summed, s.back(SLOTS).n + 1)
                    pool.wait_ge(layer.index_copied, s.n + 1)
                    pool.sem_inc(pool_may_go, 1)
                    for j in range(2):
                        pool.indirect_dma_start(nbr[s.slot][:, j, 0:width], None, table,
                                                bass.IndirectOffsetOnAxis(gather_at[s.slot][:, j:j + 1], axis=0),
                                                bounds_check=last_row, oob_is_err=False
                                                ).then_inc(layer.gathered[s.slot], 16)

                def step(s):
                    gather(s)
                    if layer is not L1:
                        return
                    t = s.back(7)
                    if t.live():
                        pool.wait_ge(L1.h2_hi_ready, t.n + 1)
                        if t.has(2):
                            pool.wait_ge(L1.dense_done, t.back(2).n + 1)
                        pool.sem_inc(pool_may_go, 1)
                        pool.tensor_tensor(h2_lo[t.half][:, :, :], h2[t.half][:, :, :],
                                           h2_hi[t.half][:, :, :].bitcast(FP32), ALU.subtract
                                           ).then_inc(L1.h2_lo_ready, 1)
                    t = s.back(9)
                    if t.live():
                        pool.wait_ge(L1.y_mid_ready, t.n + 1)
                        pool.wait_ge(L1.x_loaded[t.slot], (t.use + 1) * 16)
                        if t.has(SLOTS):
                            pool.wait_ge(L1.stored[t.slot], t.use * 32)
                        pool.sem_inc(pool_may_go, 1)
                        pool.tensor_tensor(y_out[t.slot][:, :, :], y_mid[t.half][:, :, :], x_in[t.slot][:, :, :],
                                           ALU.add).then_inc(L1.rows_ready, 1)
                if layer is L1:
                    pipeline(pool, step, PAIRS, 9, rounds=3)
                else:
                    pipeline(pool, step, PAIRS, 0)

            def gather_pass(layer, pass_no):
                table, sums, width = GENERAL[pass_no]
                with pool.If(pool.value_load(general_flag[0:1, 0:1], min_val=0, max_val=1) != 0):
                    gathers(layer, sums, width)
                with pool.Else():
                    gathers(layer, table, width)

            pool.wait_ge(flag_set, 1)
            pool.wait_ge(tables_ready, 1)
            for q in range(SLOTS):
                pool.memset(nbr[q][:, :, :], 0.0).then_inc(nbr_cleared, 1)
            pool.wait_ge(nbr_cleared, SLOTS)
            for q in range(SLOTS):
                pool.memset(nbr[q][:, :, D:D + 1], 1.0).then_inc(nbr_cleared, 1)
            all_stored(pool, h0_stored, GROUPS // NORM_SLOTS)
            general(0)
            gather_pass(L0, 0)
            all_stored(pool, L0.stored, SLOT_USES)
            general(1)
            gather_pass(L1, 1)
            all_stored(pool, L1.stored, 2 * SLOT_USES)
            general(2)
            gather_pass(L2, 2)

        @block.scalar
        def _(act):
            act.wait_ge(const_made, 1)
            act.wait_ge(w_loaded, 16 * 9)
            act.activation(w_hi[:, :, :], weights[:, :, :], ACT.Copy).then_inc(w_hi_ready, 1)

            def norm_step(s):
                if s.live():
                    act.wait_ge(moments_ready, s.n + 1)
                    act.activation(std[s.slot][:, :], moments[s.slot][:, :, 1], ACT.Sqrt, bias=eps_col[:, :]
                                   ).then_inc(std_ready, 1)
                t = s.back(1)
                if t.live():
                    act.wait_ge(norm_ready, t.n + 1)
                    for j in range(4):
                        last = act.activation(norm_rows[t.slot][:, j, :], norm_rows[t.slot][:, j, :], ACT.Relu,
                                              bias=shift[t.slot][:, j:j + 1], scale=rstd[t.slot][:, j:j + 1])
                    last.then_inc(h0_ready, 1)
                u = s.back(2)
                if u.live():
                    act.wait_ge(h0_ready, u.n + 1)
                    act.dma_start(group_rows(h0_dram, u), norm_rows[u.slot][:, :, :]).then_inc(h0_stored[u.slot], 16)
            pipeline(act, norm_step, GROUPS, 2, slots=NORM_SLOTS)

            def scale_own(layer, s, width):
                if not s.live():
                    return
                act.wait_ge(layer.own_loaded[s.slot], (s.use + 1) * 16)
                if layer is L0:
                    act.wait_ge(L0.scale_ready, s.n + 1)
                if s.has(2):
                    act.wait_ge(layer.agg_ready, s.back(2).n + 1)
                for j in range(2):
                    last = act.activation(own_scaled[s.half][:, j, 0:width], own[s.slot][:, j, 0:width], ACT.Copy,
                                          scale=self_scale[:, bass.ds(s.n * 2 + j, 1)])
                last.then_inc(layer.own_scaled, 1)

            def cat_hi_part(layer, s, j, banks, blocks):
                act.wait_ge(layer.turned, s.n + 1)
                if s.has(2):
                    act.wait_ge(layer.dense_done if layer is L0 else layer.hid_done, s.back(2).n + 1)
                return act.activation(cat_hi[s.half][:, 0:blocks, j], banks.rearrange("p (k n) -> p k n", k=blocks),
                                      ACT.Copy)

            def layer0(s):
                t = s.back(3)
                if t.live():
                    cat_hi_part(L0, t, slice(0, PAIR), ps["turn"][t.half][:, :], 2).then_inc(L0.cat_hi_ready, 1)
                scale_own(L0, s.back(1), D)
                t = s.back(5)
                if t.live():
                    act.wait_ge(L0.dense_done, t.n + 1)
                    if t.has(SLOTS):
                        act.wait_ge(L0.stored[t.slot], t.use * 16)
                    act.activation(h1_out[t.slot][:, :, :], ps["out"][t.half][:, :].rearrange("p (j f) -> p j f", j=2),
                                   ACT.Relu).then_inc(L0.rows_ready, 1)
                u = s.back(6)
                if u.live():
                    act.wait_ge(L0.rows_ready, u.n + 1)
                    act.dma_start(pair_rows(h1_dram, u), h1_out[u.slot][:, :, :]).then_inc(L0.stored[u.slot], 16)
            pipeline(act, layer0, PAIRS, 6)

            def layer1(first):
                if first.live():
                    act.wait_ge(L1.gathered[first.slot], (first.use + 1) * 32)
                    if first.has(2):
                        act.wait_ge(L1.summed, first.back(2).n + 1)
                    act.activation(nbr_hi[first.half][:, :, :], nbr[first.slot][:, :, :], ACT.Copy
                                   ).then_inc(L1.nbr_hi_ready, 1)
                s = first.back(1)
                scale_own(L1, s, H)
                t = s.back(5)
                if t.live():
                    act.wait_ge(L1.dense_done, t.n + 1)
                    if t.has(SLOTS):
                        act.wait_ge(L1.stored[t.slot], t.use * 32)
                    act.activation(z_out[t.slot][:, :, :],
                                   ps["out"][t.half][:, :].rearrange("p (j f) -> p j f", j=2)[:, :, 0:D],
                                   ACT.Copy).then_inc(L1.z_ready, 1)
                t = s.back(1)
                if t.live():
                    for j in range(2):
                        last = cat_hi_part(L1, t, slice(j * P, (j + 1) * P), ps["turn"][j][:, :], 4)
                        last.then_inc(L1.cat_hi_ready, 1)
                u = s.back(6)
                if u.live():
                    act.wait_ge(L1.rows_ready, u.n + 1)
                    act.dma_start(pair_rows(z_dram, u), z_out[u.slot][:, :, :]).then_inc(L1.stored[u.slot], 16)
                    act.dma_start(pair_rows(y_dram, u), y_out[u.slot][:, :, :]).then_inc(L1.stored[u.slot], 16)
                t = s.back(2)
                if t.live():
                    act.wait_ge(L1.hid_done, t.n + 1)
                    if t.has(2):
                        act.wait_ge(L1.h2_lo_ready, t.back(2).n + 1)
                    for m in range(2):
                        last = act.activation(h2[t.half][:, m, :], ps["hid"][t.half][:, m * PAIR:(m + 1) * PAIR],
                                              ACT.Relu, bias=b1_col[:, m:m + 1])
                    last.then_inc(L1.h2_made, 1)
            pipeline(act, layer1, PAIRS, 7)

            def layer2(s):
                u = s.back(1)
                if u.live():
                    act.wait_ge(L2.rows_ready, u.n + 1)
                    act.dma_start(pair_rows(out, u), y_out[u.slot][:, :, :]).then_inc(L2.stored[u.slot], 16)
            pipeline(act, layer2, PAIRS, 1)

        @block.vector
        def _(dve):
            dve.wait_ge(iota_made, 3)
            dve.tensor_copy(iota_row[:, :], iota_row_i[:, :])
            dve.tensor_copy(iota_col[:, :], iota_col_i[:, :])
            dve.tensor_copy(tile_base[:, :], tile_base_i[:, :])
            dve.memset(ones[:, :], 1.0)
            dve.memset(ones3[:, :], 1.0)
            dve.memset(faults[:, :], 0.0)
            dve.memset(base_degree[:, :], 1.0)
            dve.memset(eps_col[:, :], EPS).then_inc(const_made, 1)
            dve.wait_ge(const_made, 1)
            dve.tensor_scalar(ident[:, :], iota_row[:, :], iota_col[:, 0:1], None, op0=ALU.is_equal
                              ).then_inc(const_made, 1)
            done = [0]

            def own_step(ins):
                done[0] += 1
                ins.then_inc(prep, 1)
                dve.wait_ge(prep, done[0])

            dve.wait_ge(dst_loaded, 32)
            dve.tensor_copy(samples[:, :], dst_all[:, :].rearrange("p (r w) -> p r w", w=ROW)[:, :, 0]
                            ).then_inc(sampled, 1)
            own_step(dve.tensor_tensor(scratch_rows[0:EP, 0:EW - 1], dst_all[:, 0:EW - 1], dst_all[:, 1:EW],
                                       ALU.is_gt))
            dve.reduce_sum(faults[0:EP, 0:1], scratch_rows[0:EP, 0:EW - 1], AX.X)
            own_step(dve.tensor_tensor(faults[0:EP - 1, 1:2], dst_all[0:EP - 1, EW - 1:EW], dst_next[:, 0:1], ALU.is_gt))

            dve.wait_ge(w_loaded, 16 * 9)
            dve.tensor_copy(bias_part[:, 0, :], bias_row[:, :]).then_inc(bias_split, 1)
            dve.wait_ge(bias_split, 1)
            dve.tensor_tensor(bias_rest[:, 0, :], bias_row[:, :], bias_part[:, 0, :], ALU.subtract).then_inc(bias_split, 1)
            dve.wait_ge(bias_split, 2)
            dve.tensor_copy(bias_part[:, 1, :], bias_rest[:, 0, :]).then_inc(bias_split, 1)
            dve.wait_ge(bias_split, 3)
            dve.tensor_tensor(bias_rest[:, 1, :], bias_rest[:, 0, :], bias_part[:, 1, :], ALU.subtract
                              ).then_inc(bias_split, 1)
            dve.wait_ge(bias_split, 4)
            dve.tensor_copy(bias_part[:, 2, :], bias_rest[:, 1, :]).then_inc(bias_split, 1)

            dve.wait_ge(w_hi_ready, 1)
            dve.tensor_tensor(w_lo[:, :, :], weights[:, :, :], w_hi[:, :, :].bitcast(FP32), ALU.subtract
                              ).then_inc(w_ready, 1)

            dve.wait_ge(sample_spread, 16)
            for c in range(CHUNKS):
                own_step(dve.tensor_scalar(scratch_rows[0:TP, :], samples_b[:, :], tile_base[:, c:c + 1], None,
                                           op0=ALU.is_lt, op1=ALU.add, accum_out=below[:, c:c + 1]))
            own_step(dve.tensor_scalar(row_f[:, :], below[:, :], -1.0, 0.0, op0=ALU.add, op1=ALU.max))
            for r in range(WROWS):
                last = dve.tensor_scalar(row_index[:, r, :], row_f[:, :], float(r), None, op0=ALU.add)
            last.then_inc(rows_found, 1)

            def norm_step(s):
                if s.live():
                    dve.wait_ge(x_loaded[s.slot], (s.use + 1) * 16)
                    for j in range(4):
                        last = dve.bn_stats(stats[s.slot][:, j, :], norm_rows[s.slot][:, j, :])
                    last.then_inc(stats_done, 1)
                t = s.back(1)
                if t.live():
                    dve.wait_ge(std_ready, t.n + 1)
                    if s.live():
                        dve.wait_ge(stats_done, s.n + 1)
                    dve.reciprocal(rstd[t.slot][:, :], std[t.slot][:, :]).then_inc(recip_done, 1)
                if s.live():
                    if not t.live():
                        dve.wait_ge(stats_done, s.n + 1)
                    for j in range(4):
                        last = dve.bn_aggr(moments[s.slot][:, j, :], stats[s.slot][:, j, :])
                    last.then_inc(moments_ready, 1)
                if t.live():
                    dve.wait_ge(recip_done, t.n + 1)
                    dve.scalar_tensor_tensor(shift[t.slot][:, :], moments[t.slot][:, :, 0], -1.0, rstd[t.slot][:, :],
                                             op0=ALU.mult, op1=ALU.mult).then_inc(norm_ready, 1)
            peeled(norm_step, 0, 2 * NORM_SLOTS, GROUPS, NORM_SLOTS)
            looped(dve, norm_step, 2, NORM_BEFORE_KEYS, GROUPS, NORM_SLOTS)

            wide = [TP, CHUNKS, WIN]
            base_b = tile_base[:, :].rearrange("p (c a) -> p c a", a=1).to_broadcast(wide)
            dve.wait_ge(win_gathered, 16 * CHUNKS * WROWS * 2)
            dve.tensor_copy(wf_dst[:, :, :], win_dst[:, :, :])
            own_step(dve.tensor_copy(wf_src[:, :, :], win_src[:, :, :]))
            own_step(dve.tensor_tensor(wf_rel[:, :, :], wf_dst[:, :, :], base_b, ALU.subtract))
            own_step(dve.tensor_scalar(wf_in[:, :, :], wf_rel[:, :, :], 0.0, None, op0=ALU.is_ge))
            own_step(dve.scalar_tensor_tensor(wf_in[:, :, :], wf_rel[:, :, :], float(P), wf_in[:, :, :],
                                              op0=ALU.is_lt, op1=ALU.mult))
            dve.memset(wf_loop[:, :, WIN - 1:WIN], 0.0)
            own_step(dve.tensor_tensor(wf_loop[:, :, 0:WIN - 1], wf_dst[:, :, 0:WIN - 1], wf_dst[:, :, 1:WIN],
                                       ALU.not_equal))
            own_step(dve.tensor_tensor(wf_key[:, :, :], wf_src[:, :, :], wf_dst[:, :, :], ALU.is_equal))
            own_step(dve.tensor_tensor(wf_loop[:, :, :], wf_loop[:, :, :], wf_key[:, :, :], ALU.mult))
            own_step(dve.tensor_tensor(wf_loop[:, :, :], wf_loop[:, :, :], wf_in[:, :, :], ALU.mult))
            dve.reduce_sum(loop_count[:, :], wf_loop[:, :, :], AX.X)
            own_step(dve.tensor_tensor(wf_in[:, :, :], wf_in[:, :, :], wf_loop[:, :, :], ALU.subtract))
            own_step(dve.scalar_tensor_tensor(wf_key[:, :, :], wf_src[:, :, :], float(P), wf_rel[:, :, :],
                                              op0=ALU.mult, op1=ALU.add))
            own_step(dve.scalar_tensor_tensor(wf_key[:, :, :], wf_key[:, :, :], 1.0, wf_in[:, :, :],
                                              op0=ALU.add, op1=ALU.mult))
            own_step(dve.tensor_scalar(nodes_in[:, :], tile_base[:, :], -1.0, float(N_NODES), op0=ALU.mult, op1=ALU.add))
            own_step(dve.tensor_scalar(nodes_in[:, :], nodes_in[:, :], 0.0, float(P), op0=ALU.max, op1=ALU.min))
            own_step(dve.tensor_tensor(nodes_in[:, :], nodes_in[:, :], loop_count[:, :], ALU.not_equal))
            dve.reduce_sum(faults[0:TP, 2:3], nodes_in[:, :], AX.X)
            own_step(dve.tensor_scalar(below[:, :], wf_rel[:, :, WIN - 1], float(P), None, op0=ALU.is_lt))
            own_step(dve.reduce_sum(faults[0:TP, 3:4], below[:, :], AX.X))

            picked = done[0]
            with dve.Fori(NORM_BEFORE_KEYS, NORM_AFTER_KEYS) as i:
                r = i - NORM_BEFORE_KEYS
                for c in range(CHUNKS):
                    last = dve.max(top8[:, c, :], wf_key[:, c, :])
                last.then_inc(prep, 1)
                dve.wait_ge(prep, r * 2 + (picked + 1))
                dve.tensor_copy(keys[:, :, bass.ds(r * 8, 8)], top8[:, :, :])
                for c in range(CHUNKS):
                    last = dve.match_replace(wf_key[:, c, :], top8[:, c, :], wf_key[:, c, :], 0.0)
                last.then_inc(prep, 1)
                dve.wait_ge(prep, r * 2 + (picked + 2))
                dve.sem_inc(keys_ready, 1)
                for slot in range(NORM_SLOTS):
                    norm_step(Step(i, slot, GROUPS, True, NORM_SLOTS))
            done[0] += 2 * (P // 8)
            dve.reduce_max(faults[0:TP, 4:5], wf_key[:, :, :], AX.XY).then_inc(faults_ready, 1)
            dve.wait_ge(keys_turned, 1)
            own_step(dve.tensor_copy(keys_t[:, 0:4 * TP], ps["turn"][0][:, 0:4 * TP]))
            own_step(dve.tensor_copy(keys_t[:, 4 * TP:TILES], ps["turn"][1][:, 0:(CHUNKS - 4) * TP]))
            dve.tensor_scalar(key_i[:, :], keys_t[:, :], -1.0, None, op0=ALU.add)
            own_step(dve.tensor_scalar(empty_t[:, :], keys_t[:, :], 0.0, -float(SENTINEL), op0=ALU.is_equal,
                                       op1=ALU.mult))
            dve.tensor_scalar(slot_index[:, :], key_i[:, :], 7, None, op0=ALU.logical_shift_right)
            own_step(dve.tensor_scalar(node_i[:, :], key_i[:, :], P - 1, None, op0=ALU.bitwise_and))
            own_step(dve.tensor_tensor(slot_node[:, :], node_i[:, :], empty_t[:, :], ALU.add))
            dve.wait_ge(faults_summed, 1)
            own_step(dve.reduce_sum(fault_sum[:, :], ps["out"][0][:, 0:8], AX.X))
            dve.tensor_scalar(fast[:, :], fault_sum[:, :], 0.0, None, op0=ALU.is_equal)
            own_step(dve.tensor_scalar(general_flag[:, :], fault_sum[0:1, :], 0.0, None, op0=ALU.is_gt))
            dve.sem_inc(flag_set, 1)
            dve.sem_inc(tables_ready, 1)

            looped(dve, norm_step, NORM_AFTER_KEYS, GROUPS // NORM_SLOTS, GROUPS, NORM_SLOTS)
            peeled(norm_step, GROUPS, GROUPS + 1, GROUPS, NORM_SLOTS)

            def general(pass_no):
                table, sums, width = GENERAL[pass_no]
                with dve.If(dve.value_load(general_flag[0:1, 0:1], min_val=0, max_val=1) != 0):
                    with_degree = pass_no == 0
                    first = pass_no * EW
                    if with_degree:
                        dve.wait_ge(ge_loaded, 16)
                        dve.tensor_scalar(ge_before[:, :], iota_row[0:EP, 0:EP], iota_col[0:EP, :], None,
                                          op0=ALU.is_lt)
                    steps = 6
                    own = [0]
                    with dve.Fori(0, EW) as i:
                        def mine(ins):
                            own[0] += 1
                            ins.then_inc(ge_dve, 1)
                            dve.wait_ge(ge_dve, i * steps + (first * steps + own[0]))
                        column = dst_all[:, bass.ds(i, 1)]
                        dve.tensor_copy(ge_src[:, :], src_all[:, bass.ds(i, 1)])
                        dve.tensor_copy(ge_at[:, :], column)
                        mine(dve.tensor_copy(ge_dst[:, :], column))
                        dve.tensor_scalar(ge_dst_b[:, :], iota_row[0:EP, 0:EP], 0.0, ge_dst[:, :], op0=ALU.mult,
                                          op1=ALU.add).then_inc(ge_spread, 1)
                        dve.wait_ge(ge_turned, i + (first + 1))
                        mine(dve.tensor_scalar(ge_same[:, :], ps["hid"][1][0:EP, 0:EP], ge_dst[:, :], None,
                                               op0=ALU.is_equal))
                        dve.reduce_sum(ge_count[:, :], ge_same[:, :], AX.X)
                        mine(dve.tensor_tensor(ge_mask[:, :], ge_same[:, :], ge_before[:, :], ALU.mult))
                        mine(dve.reduce_sum(ge_dup[:, :], ge_mask[:, :], AX.X))
                        mine(dve.tensor_scalar(ge_dup[:, :], ge_dup[:, :], 0.0, float(SENTINEL), op0=ALU.is_gt,
                                               op1=ALU.mult))
                        mine(dve.tensor_tensor(ge_put_at[:, :], ge_dst[:, :], ge_dup[:, :], ALU.add))
                        dve.sem_inc(ge_index, 1)
                        dve.wait_ge(ge_summed, i + (first + 1))
                        fetches = 3 if with_degree else 2
                        dve.wait_ge(ge_fetched[pass_no], i * (16 * fetches) + 16 * fetches)
                        if with_degree:
                            dve.tensor_tensor(ge_deg_new[:, :], ge_deg[:, :], ge_count[:, :], ALU.add)
                        dve.tensor_tensor(ge_new[:, 0:width], ps["hid"][0][0:EP, 0:width], ge_cur[:, 0:width],
                                          ALU.add).then_inc(ge_new_ready, 1)
                        puts = 2 if with_degree else 1
                        dve.wait_ge(ge_put[pass_no], i * (16 * puts) + 16 * puts)
                    if with_degree:
                        dve.wait_ge(ge_base_loaded, 16)
                        dve.tensor_scalar(base_degree[:, :], ge_base[:, :], 1.0, None, op0=ALU.max)
                        dve.tensor_scalar(slot_node[:, :], ge_base[:, :], 0.0, iota_col[:, :], op0=ALU.mult,
                                          op1=ALU.add).then_inc(ge_nodes_set, 1)
                        dve.wait_ge(ge_nodes_set, 1)

            def copies_index(layer, s):
                if not s.live():
                    return
                if s.has(SLOTS):
                    dve.wait_ge(layer.gathered[s.slot], s.use * 32)
                dve.tensor_copy(gather_at[s.slot][:, :], slot_index[:, bass.ds(s.n * 2, 2)]
                                ).then_inc(layer.index_copied, 1)

            def selects(layer, s):
                if not s.live():
                    return
                if s.has(2):
                    dve.wait_ge(layer.summed, s.back(2).n + 1)
                for j in range(2):
                    last = dve.tensor_scalar(select[s.half][:, j, :], iota_row[:, :],
                                             slot_node[:, bass.ds(s.n * 2 + j, 1)], None, op0=ALU.is_equal)
                last.then_inc(layer.selected, 1)

            def means(layer, s, width, stride):
                if not s.live():
                    return
                dve.wait_ge(layer.summed, s.n + 1)
                dve.wait_ge(layer.own_scaled, s.n + 1)
                if s.has(2):
                    dve.wait_ge(layer.turned, s.back(2).n + 1)
                for j in range(2):
                    last = dve.scalar_tensor_tensor(agg[s.half][:, j, 0:width],
                                                    sum_bank(layer, s)[:, j * stride:j * stride + width],
                                                    inv_degree[:, bass.ds(s.n * 2 + j, 1)],
                                                    own_scaled[s.half][:, j, 0:width], op0=ALU.mult, op1=ALU.add)
                last.then_inc(layer.agg_ready, 1)

            general(0)

            def cat_lo_part(layer, s, j, hi_count, banks, blocks):
                dve.wait_ge(layer.cat_hi_ready, hi_count)
                if s.has(2):
                    dve.wait_ge(layer.dense_done if layer is L0 else layer.hid_done, s.back(2).n + 1)
                return dve.tensor_tensor(cat_lo[s.half][:, 0:blocks, j], banks.rearrange("p (k n) -> p k n", k=blocks),
                                         cat_hi[s.half][:, 0:blocks, j].bitcast(FP32), ALU.subtract)

            def layer0(first):
                copies_index(L0, first)
                s = first.back(5)
                means(L0, s.back(2), D, H)
                selects(L0, first.back(4))
                if s.live():
                    dve.wait_ge(L0.summed, s.n + 1)
                    two = bass.ds(s.n * 2, 2)
                    counts = sum_bank(L0, s).rearrange("p (j f) -> p j f", j=2)[:, :, D]
                    dve.scalar_tensor_tensor(degree[s.half][:, :], counts, fast[:, :], base_degree[:, two],
                                             op0=ALU.mult, op1=ALU.add).then_inc(L0.degree_done, 1)
                t = s.back(3)
                if t.live():
                    cat_lo_part(L0, t, slice(0, PAIR), t.n + 1, ps["turn"][t.half][:, :], 2
                                ).then_inc(L0.cat_ready, 1)
                if s.live():
                    dve.wait_ge(L0.degree_done, s.n + 1)
                    dve.reciprocal(inv_degree[:, two], degree[s.half][:, :]).then_inc(L0.recip_done, 1)
                    dve.wait_ge(L0.recip_done, s.n + 1)
                    dve.tensor_scalar(self_scale[:, two], inv_degree[:, two], fast[:, :], None, op0=ALU.mult
                                      ).then_inc(L0.scale_ready, 1)
            pipeline(dve, layer0, PAIRS, 8, rounds=3)

            general(1)

            def layer1(first):
                copies_index(L1, first)
                selects(L1, first.back(4))
                t = first.back(4)
                if t.live():
                    dve.wait_ge(L1.nbr_hi_ready, t.n + 1)
                    dve.tensor_tensor(nbr_lo[t.half][:, :, :], nbr[t.slot][:, :, :],
                                      nbr_hi[t.half][:, :, :].bitcast(FP32), ALU.subtract).then_inc(L1.nbr_split, 1)
                s = first.back(5)
                t = s.back(5)
                if t.live():
                    dve.wait_ge(L1.dense_done, t.n + 1)
                    dve.wait_ge(L1.z_ready, t.n + 1)
                    if t.has(2):
                        dve.wait_ge(L1.rows_ready, t.back(2).n + 1)
                    for j in range(2):
                        last = dve.scalar_tensor_tensor(y_mid[t.half][:, j, :], z_out[t.slot][:, j, :],
                                                        self_scale[:, bass.ds(t.n * 2 + j, 1)],
                                                        ps["out"][t.half][:, j * H + D:(j + 1) * H],
                                                        op0=ALU.mult, op1=ALU.add)
                    last.then_inc(L1.y_mid_ready, 1)
                t = s.back(3)
                if t.live():
                    dve.wait_ge(L1.h2_made, t.n + 1)
                    if t.has(2):
                        dve.wait_ge(L1.dense_done, t.back(2).n + 1)
                    dve.tensor_copy(h2_hi[t.half][:, :, :], h2[t.half][:, :, :]).then_inc(L1.h2_hi_ready, 1)
                means(L1, s, H, H)
                t = s.back(1)
                if t.live():
                    for j in range(2):
                        last = cat_lo_part(L1, t, slice(j * P, (j + 1) * P), t.n * 2 + (j + 1), ps["turn"][j][:, :], 4)
                    last.then_inc(L1.cat_ready, 1)
            pipeline(dve, layer1, PAIRS, 10, rounds=4)

            general(2)

            def layer2(first):
                copies_index(L2, first)
                selects(L2, first.back(4))
                s = first.back(5)
                if s.live():
                    dve.wait_ge(L2.own_loaded[s.slot], (s.use + 1) * 16)
                    dve.wait_ge(L2.summed, s.n + 1)
                    if s.has(SLOTS):
                        dve.wait_ge(L2.stored[s.slot], s.use * 16)
                    for j in range(2):
                        last = dve.scalar_tensor_tensor(y_out[s.slot][:, j, :], ps["agg"][s.half][:, j * H:j * H + D],
                                                        inv_degree[:, bass.ds(s.n * 2 + j, 1)],
                                                        own[s.slot][:, j, 0:D], op0=ALU.mult, op1=ALU.add)
                    last.then_inc(L2.rows_ready, 1)
            pipeline(dve, layer2, PAIRS, 5, rounds=3)

        @block.tensor
        def _(pe):
            pe.wait_ge(const_made, 2)
            pe.wait_ge(keys_ready, P // 8)
            for c in range(CHUNKS):
                at = (c % 4) * TP
                last = nc.tensor.matmul(ps["turn"][c // 4][:, at:at + TP], keys[:, c, :], ident[0:TP, 0:TP],
                                        is_transpose=True, start=True, stop=True)
            last.then_inc(keys_turned, 1)
            pe.wait_ge(faults_ready, 1)
            nc.tensor.matmul(ps["out"][0][:, 0:8], ones[:, :], faults[:, :], start=True, stop=True
                             ).then_inc(faults_summed, 1)

            def general(pass_no):
                table, sums, width = GENERAL[pass_no]
                with pe.If(pe.value_load(general_flag[0:1, 0:1], min_val=0, max_val=1) != 0):
                    with_degree = pass_no == 0
                    fetches = 3 if with_degree else 2
                    first = pass_no * EW
                    with pe.Fori(0, EW) as i:
                        pe.wait_ge(ge_spread, i + (first + 1))
                        nc.tensor.matmul(ps["hid"][1][0:EP, 0:EP], ge_dst_b[:, :], ident[0:EP, 0:EP],
                                         is_transpose=True, start=True, stop=True).then_inc(ge_turned, 1)
                        pe.wait_ge(ge_index, i + (first + 1))
                        pe.wait_ge(ge_fetched[pass_no], i * (16 * fetches) + 16 * fetches)
                        nc.tensor.matmul(ps["hid"][0][0:EP, 0:width], ge_same[:, :], ge_msg[:, 0:width],
                                         start=True, stop=True).then_inc(ge_summed, 1)
                    pe.wait_ge(ge_new_ready, first + EW)

            def sums(layer, s, width, stride):
                if not s.live():
                    return
                if layer is L1:
                    pe.wait_ge(L1.nbr_split, s.n + 1)
                else:
                    pe.wait_ge(layer.gathered[s.slot], (s.use + 1) * 32)
                pe.wait_ge(layer.selected, s.n + 1)
                banks = SLOTS if layer is L0 else 2
                if s.has(banks):
                    pe.wait_ge(layer.rows_ready if layer is L2 else layer.agg_ready, s.back(banks).n + 1)
                for j in range(2):
                    o = sum_bank(layer, s)[:, j * stride:j * stride + width]
                    if layer is L1:
                        nc.tensor.matmul(o, select[s.half][:, j, :], nbr_hi[s.half][:, j, :], start=True, stop=False)
                        last = nc.tensor.matmul(o, select[s.half][:, j, :], nbr_lo[s.half][:, j, :],
                                                start=False, stop=True)
                    else:
                        last = nc.tensor.matmul(o, select[s.half][:, j, :].bitcast(FP32), nbr[s.slot][:, j, 0:width],
                                                start=True, stop=True)
                last.then_inc(layer.summed, 1)

            pe.wait_ge(w_ready, 1)
            pe.wait_ge(bias_moved, 16 * 3)
            pe.wait_ge(flag_set, 1)
            pe.wait_ge(nbr_cleared, 2 * SLOTS)
            general(0)

            def product(o, pairs, first=True, last=True):
                terms = [t for (a_hi, a_lo), (b_hi, b_lo) in pairs
                         for t in ((a_hi, b_hi), (a_hi, b_lo), (a_lo, b_hi))]
                for n, (a, b) in enumerate(terms):
                    ins = nc.tensor.matmul(o, a, b, start=first and n == 0, stop=last and n == len(terms) - 1)
                return ins

            def layer0(s):
                sums(L0, s, D + 1, H)
                t = s.back(4)
                if t.live():
                    pe.wait_ge(L0.cat_ready, t.n + 1)
                    if t.has(2):
                        pe.wait_ge(L0.rows_ready, t.back(2).n + 1)
                    for j in range(2):
                        o = ps["out"][t.half][:, j * H:(j + 1) * H]
                        nodes = slice(j * P, (j + 1) * P)
                        nc.tensor.matmul(o, ones3[:, :], bias3[:, 0:H], start=True, stop=False)
                        last = product(o, [((cat_hi[t.half][:, k, nodes], cat_lo[t.half][:, k, nodes]),
                                            (w_hi[:, W0 + k, :], w_lo[:, W0 + k, :])) for k in range(2)], first=False)
                    last.then_inc(L0.dense_done, 1)
                t = s.back(2)
                if t.live():
                    pe.wait_ge(L0.agg_ready, t.n + 1)
                    pe.wait_ge(L0.own_loaded[t.slot], (t.use + 1) * 16)
                    if t.has(2):
                        pe.wait_ge(L0.cat_ready, t.back(2).n + 1)
                    for j in range(2):
                        for k, rows in enumerate((own[t.slot], agg[t.half])):
                            at = k * PAIR + j * P
                            last = nc.tensor.matmul(ps["turn"][t.half][:, at:at + P], rows[:, j, 0:D], ident[:, :],
                                                    is_transpose=True, start=True, stop=True)
                    last.then_inc(L0.turned, 1)
            pipeline(pe, layer0, PAIRS, 4)

            general(1)

            def layer1(s):
                sums(L1, s, H, H)
                t = s.back(1)
                if t.live():
                    pe.wait_ge(L1.agg_ready, t.n + 1)
                    pe.wait_ge(L1.own_loaded[t.slot], (t.use + 1) * 16)
                    if t.has(1):
                        pe.wait_ge(L1.cat_ready, t.back(1).n + 1)
                    for j in range(2):
                        for k in range(4):
                            rows = (own[t.slot], agg[t.half])[k // 2][:, j, (k % 2) * P:(k % 2 + 1) * P]
                            last = nc.tensor.matmul(ps["turn"][j][:, k * P:(k + 1) * P], rows, ident[:, :],
                                                    is_transpose=True, start=True, stop=True)
                    last.then_inc(L1.turned, 1)
                t = s.back(2)
                if t.live():
                    pe.wait_ge(L1.cat_ready, t.n + 1)
                    if t.has(2):
                        pe.wait_ge(L1.h2_made, t.back(2).n + 1)
                    for m in range(2):
                        out_features = slice(m * P, (m + 1) * P)
                        last = product(ps["hid"][t.half][:, m * PAIR:(m + 1) * PAIR],
                                       [((w_hi[:, W1 + k, out_features], w_lo[:, W1 + k, out_features]),
                                         (cat_hi[t.half][:, k, :], cat_lo[t.half][:, k, :])) for k in range(4)])
                    last.then_inc(L1.hid_done, 1)
                t = s.back(4)
                if t.live():
                    pe.wait_ge(L1.h2_lo_ready, t.n + 1)
                    if t.has(2):
                        pe.wait_ge(L1.z_ready, t.back(2).n + 1)
                        pe.wait_ge(L1.y_mid_ready, t.back(2).n + 1)
                    for j in range(2):
                        o = ps["out"][t.half][:, j * H:(j + 1) * H]
                        nodes = slice(j * P, (j + 1) * P)
                        product(o, [((h2_hi[t.half][:, m, nodes], h2_lo[t.half][:, m, nodes]),
                                     (w_hi[:, W2 + m, :], w_lo[:, W2 + m, :])) for m in range(2)], last=False)
                        last = nc.tensor.matmul(o[:, D:2 * D], ones3[:, :], bias3[:, H:H + D], start=False, stop=True)
                    last.then_inc(L1.dense_done, 1)
            pipeline(pe, layer1, PAIRS, 4)

            general(2)
            pipeline(pe, lambda s: sums(L2, s, D, H), PAIRS, 0)


INPUTS = ["x", "src", "dst", "L0_gnn_ws0", "L0_gnn_wn0", "L0_gnn_b0", "L0_gnn_ws1", "L0_gnn_wn1", "L0_gnn_b1",
          "L0_gnn_ws2", "L0_gnn_wn2", "L0_gnn_b2"]


def kernel(**inputs):
    import numpy as np
    import concourse.bacc as bacc
    from concourse.bass_utils import run_bass_kernel_spmd

    nc = bacc.Bacc("TRN2", target_bir_lowering=False, num_devices=1)
    arrays, args = {}, []
    for name in INPUTS:
        a = np.ascontiguousarray(inputs[name])
        if name == "x":
            padded = np.zeros((N_PAD, D), a.dtype)
            padded[:N_NODES] = a
            a = padded
        arrays[f"in_{name}"] = a
        args.append(nc.dram_tensor(f"in_{name}", a.shape, mybir.dt.from_np(a.dtype), kind="ExternalInput").ap())
    out = nc.dram_tensor("out_rows", (N_PAD, D), FP32, kind="ExternalOutput").ap()
    build(nc, *args, out)
    r = run_bass_kernel_spmd(nc, [arrays], core_ids=[0])
    return r.results[0]["out_rows"][:N_NODES]
```

```python
import concourse.bass as bass
from concourse import mybir
from contextlib import ExitStack

FP32 = mybir.dt.float32
FP32R = mybir.dt.float32r
I32 = mybir.dt.int32
ALU = mybir.AluOpType
ACT = mybir.ActivationFunctionType
AX = mybir.AxisListType

P = 128
N_NODES = 100000
N_EDGES = 150000
D = 128
H = 256
PAIR = 2 * P
SLOTS = 4
PAIRS = -(-N_NODES // (PAIR * SLOTS)) * SLOTS
TILES = 2 * PAIRS
N_PAD = TILES * P
GROUP = 4 * P
GROUPS = N_PAD // GROUP
CHUNKS = 7
TP = TILES // CHUNKS
ROW = 120
ROWS = N_EDGES // ROW
WROWS = 3
WIN = WROWS * ROW
EP = 125
EW = N_EDGES // EP
SENTINEL = 1 << 20
EPS = 1e-5
NORM_SLOTS = 7
NORM_BEFORE_KEYS = 3
NORM_AFTER_KEYS = NORM_BEFORE_KEYS + P // 8
L1_SPLIT = 1
LAYER_MEM = 5 * CHUNKS * WIN


class Step:

    def __init__(self, use, slot, total, looped, slots):
        self.use, self.slot, self.total, self.looped, self.slots = use, slot, total, looped, slots
        self.n = use * slots + slot if not looped or slot else use * slots
        self.half = slot % 2

    def back(self, lag):
        at = self.slot - lag
        rounds = at // self.slots
        return Step(self.use + rounds if rounds else self.use, at % self.slots, self.total, self.looped, self.slots)

    def live(self):
        return self.looped or 0 <= self.n < self.total

    def has(self, earlier):
        return self.looped or self.n >= earlier


def peeled(step, first, last, total, slots=SLOTS):
    for n in range(first, last):
        step(Step(n // slots, n % slots, total, False, slots))


def looped(eng, step, first_use, last_use, total, slots=SLOTS):
    with eng.Fori(first_use, last_use) as i:
        for slot in range(slots):
            step(Step(i, slot, total, True, slots))


def pipeline(eng, step, total, lag, rounds=2, slots=SLOTS):
    assert lag < rounds * slots and total % slots == 0
    peeled(step, 0, rounds * slots, total, slots)
    looped(eng, step, rounds, total // slots, total, slots)
    peeled(step, total, total + lag, total, slots)


def build(nc, x, src, dst, ws0, wn0, b0, ws1, wn1, b1, ws2, wn2, b2, out):
    h0_dram = nc.dram_tensor("h0_rows", [N_PAD, D], FP32).ap()
    p_dram = nc.dram_tensor("p_rows", [N_PAD, H], FP32).ap()
    q_dram = nc.dram_tensor("q_rows", [N_PAD, H], FP32).ap()
    z_dram = nc.dram_tensor("z_rows", [N_PAD, D], FP32).ap()
    h0_sums = nc.dram_tensor("h0_sums", [N_PAD, D], FP32).ap()
    p_sums = nc.dram_tensor("p_sums", [N_PAD, H], FP32).ap()
    z_sums = nc.dram_tensor("z_sums", [N_PAD, D], FP32).ap()
    y_dram = nc.dram_tensor("y_rows", [N_PAD, D], FP32).ap()
    samples_dram = nc.dram_tensor("dst_samples", [EP, EW // ROW], FP32).ap()
    degree_dram = nc.dram_tensor("general_degrees", [N_PAD, 1], FP32).ap()

    src_rows = src.rearrange("(r w) -> r w", w=ROW)
    dst_rows = dst.rearrange("(r w) -> r w", w=ROW)
    src_flat = src.rearrange("(p w) -> p w", w=EW)
    dst_flat = dst.rearrange("(p w) -> p w", w=EW)

    with ExitStack() as ctx:
        def sb(name, shape, dt=FP32):
            return ctx.enter_context(nc.sbuf_tensor(name, shape, dt))

        def sem(name):
            return ctx.enter_context(nc.semaphore(name))

        def sems(name, n=SLOTS):
            return [sem(f"{name}{i}") for i in range(n)]

        iota_row = sb("iota_row", [P, P])
        iota_col = sb("iota_col", [P, 1])
        iota_row_i = sb("iota_row_i", [P, P], I32)
        iota_col_i = sb("iota_col_i", [P, 1], I32)
        ident = sb("ident", [P, P])
        ones = sb("ones", [P, P])
        eps_col = sb("eps_col", [P, 1])
        w_hi = sb("w_hi", [P, 8, H], FP32R)
        w_lo = sb("w_lo", [P, 8, H], FP32R)
        W0, W1, W2 = 0, 2, 6
        b0_col = sb("b0_col", [P, 2])
        b1_rows = sb("b1_rows", [P, H])
        b2_rows = sb("b2_rows", [P, D])

        slot_index = sb("slot_index", [P, TILES], I32)
        slot_node = sb("slot_node", [P, TILES])
        base_degree = sb("base_degree", [P, TILES])
        inv_degree = sb("inv_degree", [P, TILES])
        self_scale = sb("self_scale", [P, TILES])
        fast = sb("fast", [P, 1])
        general_flag = sb("general_flag", [1, 1], I32)

        layer_mem = sb("layer_mem", [P, LAYER_MEM])
        taken = [0]

        def part(a, b):
            at = taken[0]
            taken[0] += a * b
            assert taken[0] <= LAYER_MEM
            return layer_mem[:, at:at + a * b].rearrange("p (a b) -> p a b", a=a)

        weights = layer_mem[:, 0:8 * H].rearrange("p (k n) -> p k n", k=8)

        dst_all = sb("dst_all", [EP, EW], I32)
        dst_next = sb("dst_next", [EP - 1, 2], I32)
        samples = sb("samples", [EP, EW // ROW])
        samples_b = sb("samples_b", [TP, ROWS])
        scratch_rows = sb("scratch_rows", [P, ROWS])
        tile_base_i = sb("tile_base_i", [TP, CHUNKS], I32)
        tile_base = sb("tile_base", [TP, CHUNKS])
        below = sb("below", [TP, CHUNKS])
        row_f = sb("row_f", [TP, CHUNKS])
        row_index = sb("row_index", [TP, WROWS, CHUNKS], I32)
        win_dst = sb("win_dst", [TP, CHUNKS, WIN], I32)
        win_src_mem = sb("win_src_mem", [P, CHUNKS * WIN], I32)
        win_src = win_src_mem[0:TP, :].rearrange("p (c w) -> p c w", c=CHUNKS)
        wf_dst, wf_src, wf_rel, wf_in, wf_loop = (
            layer_mem[0:TP, i * CHUNKS * WIN:(i + 1) * CHUNKS * WIN].rearrange("p (c w) -> p c w", c=CHUNKS)
            for i in range(5))
        wf_key_mem = sb("wf_key_mem", [P, CHUNKS * WIN])
        wf_key = wf_key_mem[0:TP, :].rearrange("p (c w) -> p c w", c=CHUNKS)
        loop_count = sb("loop_count", [TP, CHUNKS])
        nodes_in = sb("nodes_in", [TP, CHUNKS])
        top8 = sb("top8", [TP, CHUNKS, 8])
        keys = sb("keys", [TP, CHUNKS, P])
        keys_t = sb("keys_t", [P, TILES])
        empty_t = sb("empty_t", [P, TILES])
        key_i = sb("key_i", [P, TILES], I32)
        node_i = sb("node_i", [P, TILES], I32)
        faults = sb("faults", [P, 8])
        fault_sum = sb("fault_sum", [P, 1])

        loaded_rows = [sb(f"loaded_rows{i}", [P, 2 * H]) for i in range(SLOTS)]
        stored_rows = [sb(f"stored_rows{i}", [P, 2 * H]) for i in range(SLOTS)]
        norm_rows = [t[:, :].rearrange("p (j f) -> p j f", j=4) for t in (loaded_rows + stored_rows)[:NORM_SLOTS]]
        stats = [sb(f"stats{i}", [P, 4, 6]) for i in range(NORM_SLOTS)]
        moments = [sb(f"moments{i}", [P, 4, 2]) for i in range(NORM_SLOTS)]
        std = [sb(f"std{i}", [P, 4]) for i in range(NORM_SLOTS)]
        rstd = [sb(f"rstd{i}", [P, 4]) for i in range(NORM_SLOTS)]
        shift = [sb(f"shift{i}", [P, 4]) for i in range(NORM_SLOTS)]

        own = [t[:, :].rearrange("p (j f) -> p j f", j=2) for t in loaded_rows]
        nbr = [part(2, H) for i in range(SLOTS)]
        nbr_hi = [sb(f"nbr_hi{i}", [P, 2, H], FP32R) for i in range(2)]
        nbr_lo = [sb(f"nbr_lo{i}", [P, 2, H], FP32R) for i in range(2)]
        gather_at = [sb(f"gather_at{i}", [P, 2], I32) for i in range(SLOTS)]
        select = [sb(f"select{i}", [P, 2, P], FP32R) for i in range(2)]
        degree = [sb(f"degree{i}", [P, 2]) for i in range(2)]
        own_scaled = [part(2, D) for i in range(2)]
        agg = [part(2, H) for i in range(2)]
        cat_hi = [sb(f"cat_hi{i}", [P, 2, PAIR], FP32R) for i in range(2)]
        cat_lo = [sb(f"cat_lo{i}", [P, 2, PAIR], FP32R) for i in range(2)]
        h1 = [part(2, PAIR) for i in range(2)]
        hid_hi = [sb(f"hid_hi{i}", [P, 2, PAIR], FP32R) for i in range(2)]
        hid_lo = [sb(f"hid_lo{i}", [P, 2, PAIR], FP32R) for i in range(2)]
        p_out = [t[:, :].rearrange("p (j f) -> p j f", j=2) for t in stored_rows]
        q_out = [part(2, H) for i in range(SLOTS)]
        q_part = [part(2, H) for i in range(2)]
        z_out = [part(2, D) for i in range(SLOTS)]
        y_out = [part(2, D) for i in range(SLOTS)]
        x_in = [part(2, D) for i in range(SLOTS)]
        distance = [part(2, P) for i in range(2)]
        y_plus_sums = [part(2, D) for i in range(2)]
        x_plus_b2 = [part(2, D) for i in range(2)]

        src_all = win_src_mem[0:EP, 0:EW]
        ge_base = keys_t
        ge_taken = [0]

        def ge_part(rows, width):
            at = ge_taken[0]
            ge_taken[0] += width
            assert ge_taken[0] <= CHUNKS * WIN
            return wf_key_mem[0:rows, at:at + width]

        zero_rows = ge_part(P, 4 * H)
        ge_dst_b = ge_part(EP, EP)
        ge_same = ge_part(EP, EP)
        ge_before = ge_part(EP, EP)
        ge_mask = ge_part(EP, EP)
        ge_msg = ge_part(EP, H)
        ge_cur = ge_part(EP, H)
        ge_new = ge_part(EP, H)
        ge_src = sb("ge_src", [EP, 1], I32)
        ge_at = sb("ge_at", [EP, 1], I32)
        ge_put_at = sb("ge_put_at", [EP, 1], I32)
        ge_dst = sb("ge_dst", [EP, 1])
        ge_dup = sb("ge_dup", [EP, 1])
        ge_count = sb("ge_count", [EP, 1])
        ge_deg = sb("ge_deg", [EP, 1])
        ge_deg_new = sb("ge_deg_new", [EP, 1])

        ps = {k: [ctx.enter_context(nc.psum_tensor(f"ps_{k}{i}", [P, 512], FP32)) for i in range(2)]
              for k in ("agg", "turn", "hid", "out")}

        w_loaded, bias_loaded = sem("w_loaded"), sem("bias_loaded")
        iota_made, const_made = sem("iota_made"), sem("const_made")
        w_hi_ready, w_ready = sem("w_hi_ready"), sem("w_ready")
        dst_loaded, sampled, sample_stored, sample_spread = (
            sem("dst_loaded"), sem("sampled"), sem("sample_stored"), sem("sample_spread"))
        rows_found, win_cleared, win_gathered = sem("rows_found"), sem("win_cleared"), sem("win_gathered")
        prep = sem("prep")
        keys_ready, keys_turned = sem("keys_ready"), sem("keys_turned")
        faults_ready, faults_summed, flag_set = sem("faults_ready"), sem("faults_summed"), sem("flag_set")
        tables_ready = sem("tables_ready")
        nbr_cleared = sem("nbr_cleared")

        x_loaded, stats_done, moments_ready = sems("x_loaded", NORM_SLOTS), sem("stats_done"), sem("moments_ready")
        std_ready, recip_done, norm_ready = sem("std_ready"), sem("recip_done"), sem("norm_ready")
        h0_ready, h0_stored = sem("h0_ready"), sems("h0_stored", NORM_SLOTS)

        class Layer:

            def __init__(self, n):
                self.own_loaded = sems(f"own_loaded_{n}_")
                self.index_copied = sem(f"index_copied_{n}")
                self.gathered = sems(f"gathered_{n}_")
                self.selected = sem(f"selected_{n}")
                if n == 1:
                    self.distance_made = sem("distance_made")
                self.summed = sem(f"summed_{n}")
                self.rows_ready = sem(f"rows_ready_{n}")
                self.stored = sems(f"stored_{n}_")
                if n < 2:
                    self.nbr_hi_ready = sem(f"nbr_hi_ready_{n}")
                    self.nbr_split = sem(f"nbr_split_{n}")
                    self.agg_ready = sem(f"agg_ready_{n}")
                    self.turned = sem(f"turned_{n}")
                    self.hi_ready = sem(f"turned_hi_ready_{n}")
                    self.lo_ready = sem(f"turned_lo_ready_{n}")
                    self.dense_done = sem(f"dense_done_{n}")
                if n == 0:
                    self.own_scaled = sem("own_scaled_done")
                    self.degree_done = sem("degree_done")
                    self.recip_done = sem("inv_degree_done")
                    self.scale_ready = sem("scale_ready")
                    self.hid_done = sem("hid_done")
                    self.h1_made = sem("h1_made")
                    self.h1_hi_ready = sem("h1_hi_ready")
                    self.h1_lo_ready = sem("h1_lo_ready")
                    self.p_ready = sem("p_ready")
                    self.q_part_ready = sem("q_part_ready")
                if n == 1:
                    self.z_ready = sem("z_ready")
                if n == 2:
                    self.x_loaded = sems("x_in_loaded")
                    self.y_added = sem("y_added")

        sp_may_load = sem("sp_may_load")
        pool_may_go = sem("pool_may_go")

        L0, L1, L2 = Layer(0), Layer(1), Layer(2)

        ge_loaded, ge_zeroed = sem("ge_loaded"), sem("ge_zeroed")
        ge_dve, ge_spread, ge_turned, ge_index = sem("ge_dve"), sem("ge_spread"), sem("ge_turned"), sem("ge_index")
        ge_fetched, ge_summed, ge_new_ready, ge_put = (
            sems("ge_fetched", 3), sem("ge_summed"), sem("ge_new_ready"), sems("ge_put", 3))
        ge_zero_made, ge_base_loaded, ge_index_set = sem("ge_zero_made"), sem("ge_base_loaded"), sem("ge_index_set")
        ge_cleared = sem("ge_cleared")
        ge_nodes_set = sem("ge_nodes_set")

        def pair_rows(table, s):
            return table[bass.ds(s.n * PAIR, PAIR), :].rearrange("(j p) f -> p j f", p=P)

        def group_rows(table, s):
            return table[bass.ds(s.n * GROUP, GROUP), :].rearrange("(p j) f -> p j f", p=P)

        def sum_bank(layer, s):
            return (ps["agg"] + ps["hid"])[s.half if layer is L0 else s.slot][:, :]

        def out_bank(j):
            return ps["out"][j][:, :]

        def all_stored(eng, stored, per_slot):
            for one in stored:
                eng.wait_ge(one, per_slot * 16)

        SLOT_USES = PAIRS // SLOTS
        GENERAL = [(h0_dram, h0_sums, D), (p_dram, p_sums, H), (z_dram, z_sums, D)]
        ZERO_ROWS = 4 * P

        block = ctx.enter_context(nc.Block())

        @block.sync
        def _(sp):
            sp.dma_start(dst_all[:, :], dst_flat).then_inc(dst_loaded, 16)
            sp.dma_start(dst_next[:, :], dst_flat[1:EP, 0:2]).then_inc(dst_loaded, 16)
            sp.dma_start(b0_col[:, :], b0.rearrange("(m p) -> p m", p=P), allow_slow_non_contiguous=True).then_inc(w_loaded, 16)
            sp.dma_start(weights[:, W0, :], ws0).then_inc(w_loaded, 16)
            sp.dma_start(weights[:, W0 + 1, :], wn0).then_inc(w_loaded, 16)
            w1 = weights[:, W1:W1 + 4, :].rearrange("p (m t) n -> p t m n", t=2)
            sp.dma_start(w1[:, 0], wn1.rearrange("(m p) n -> p m n", p=P)).then_inc(w_loaded, 16)
            sp.dma_start(w1[:, 1], ws1.rearrange("(m p) n -> p m n", p=P)).then_inc(w_loaded, 16)
            sp.dma_start(weights[:, W2:W2 + 2, 0:D], wn2.rearrange("(k p) n -> p k n", p=P)).then_inc(w_loaded, 16)
            sp.dma_start(weights[:, W2:W2 + 2, D:2 * D], ws2.rearrange("(k p) n -> p k n", p=P)).then_inc(w_loaded, 16)
            for rows, b in ((b1_rows, b1), (b2_rows, b2)):
                sp.dma_start(rows[:, :], b.rearrange("(a n) -> a n", a=1).to_broadcast([P, b.shape[0]])
                             ).then_inc(bias_loaded, 16)
            sp.wait_ge(sampled, 1)
            sp.dma_start(samples_dram, samples[:, :]).then_inc(sample_stored, 16)
            sp.wait_ge(sample_stored, 16)
            sp.dma_start(samples_b[:, :], samples_dram.rearrange("(a p) w -> a (p w)", a=1).to_broadcast([TP, ROWS])
                         ).then_inc(sample_spread, 16)

            def load_x(s):
                if not s.live():
                    return
                if s.has(NORM_SLOTS):
                    sp.wait_ge(h0_stored[s.slot], s.use * 16)
                    sp.sem_inc(sp_may_load, 1)
                sp.dma_start(norm_rows[s.slot][:, :, :], group_rows(x, s)).then_inc(x_loaded[s.slot], 16)
            pipeline(sp, load_x, GROUPS, 0, slots=NORM_SLOTS)

            def general(pass_no):
                table, sums, width = GENERAL[pass_no]
                with sp.If(sp.value_load(general_flag[0:1, 0:1], min_val=0, max_val=1) != 0):
                    if pass_no == 0:
                        sp.dma_start(src_all[:, :], src_flat).then_inc(ge_loaded, 16)
                        sp.wait_ge(ge_zero_made, 1)
                        sp.dma_start(degree_dram.rearrange("(a p c) o -> a p (c o)", a=1, p=P)[0],
                                     zero_rows[:, 0:TILES]).then_inc(ge_zeroed, 16)
                        sp.wait_ge(ge_zeroed, 16)
                    done = [1, 1 + GROUPS, 1 + 2 * GROUPS][pass_no]
                    with sp.Fori(0, GROUPS) as i:
                        sp.dma_start(sums[bass.ds(i * ZERO_ROWS, ZERO_ROWS), :]
                                     .rearrange("(p j) f -> p (j f)", p=P),
                                     zero_rows[:, 0:4 * width]).then_inc(ge_zeroed, 16)
                        sp.wait_ge(ge_zeroed, i * 16 + (done + 1) * 16)
                        sp.sem_inc(sp_may_load, 1)
                    sp.sem_inc(ge_cleared, 1)
                    if pass_no == 0:
                        sp.wait_ge(ge_put[0], 16 * 2 * EW)
                        sp.dma_start(ge_base[:, :], degree_dram.rearrange("(t p) o -> p (t o)", p=P),
                                     allow_slow_non_contiguous=True
                                     ).then_inc(ge_base_loaded, 16)

            def load_own(layer, table, width, s, freed):
                if not s.live():
                    return
                if s.has(SLOTS):
                    sp.wait_ge(freed, s.back(SLOTS).n + 1)
                    sp.sem_inc(sp_may_load, 1)
                sp.dma_start(own[s.slot][:, :, 0:width], pair_rows(table, s)).then_inc(layer.own_loaded[s.slot], 16)

            sp.wait_ge(flag_set, 1)
            all_stored(sp, h0_stored, GROUPS // NORM_SLOTS)
            general(0)
            pipeline(sp, lambda s: load_own(L0, h0_dram, D, s, L0.turned), PAIRS, 0)

            all_stored(sp, L0.stored, 2 * SLOT_USES)
            general(1)

            def layer1_transfers(s):
                load_own(L1, q_dram, H, s, L1.agg_ready)
                t = s.back(8)
                if t.live():
                    sp.wait_ge(L1.rows_ready, t.n + 1)
                    sp.sem_inc(sp_may_load, 1)
                    sp.dma_start(pair_rows(z_dram, t), z_out[t.slot][:, :, :]).then_inc(L1.stored[t.slot], 16)
                    sp.dma_start(pair_rows(y_dram, t), y_out[t.slot][:, :, :]).then_inc(L1.stored[t.slot], 16)
            pipeline(sp, layer1_transfers, PAIRS, 8, rounds=3)

            all_stored(sp, L1.stored, 2 * SLOT_USES)
            general(2)

            def layer2_loads(s):
                if s.live() and s.has(SLOTS):
                    sp.wait_ge(L2.rows_ready, s.back(SLOTS).n + 1)
                    sp.sem_inc(sp_may_load, 1)
                sp.dma_start(own[s.slot][:, :, 0:D], pair_rows(y_dram, s)).then_inc(L2.own_loaded[s.slot], 16)
                sp.dma_start(x_in[s.slot][:, :, :], pair_rows(x, s)).then_inc(L2.x_loaded[s.slot], 16)
            pipeline(sp, layer2_loads, PAIRS, 0)
            all_stored(sp, L2.stored, SLOT_USES)

        @block.gpsimd
        def _(pool):
            pool.iota(iota_row_i[:, :], pattern=[[1, P]], base=0, channel_multiplier=0).then_inc(iota_made, 1)
            pool.iota(iota_col_i[:, :], pattern=[[0, 1]], base=0, channel_multiplier=1).then_inc(iota_made, 1)
            pool.iota(tile_base_i[:, :], pattern=[[P * TP, CHUNKS]], base=0, channel_multiplier=P
                      ).then_inc(iota_made, 1)
            pool.memset(win_dst[:, :, :], SENTINEL).then_inc(win_cleared, 1)
            pool.memset(win_src[:, :, :], 0).then_inc(win_cleared, 1)
            pool.wait_ge(win_cleared, 2)
            pool.wait_ge(rows_found, 1)
            for c in range(CHUNKS):
                for r in range(WROWS):
                    for rows, win in ((dst_rows, win_dst), (src_rows, win_src)):
                        pool.indirect_dma_start(win[:, c, r * ROW:(r + 1) * ROW], None, rows,
                                                bass.IndirectOffsetOnAxis(row_index[:, r, c:c + 1], axis=0),
                                                bounds_check=ROWS - 1, oob_is_err=False).then_inc(win_gathered, 16)

            limit = pool.alloc_register("last_row")
            pool.reg_mov(limit, N_PAD - 1)
            last_row = pool.snap(limit)

            def general(pass_no):
                table, sums, width = GENERAL[pass_no]
                with pool.If(pool.value_load(general_flag[0:1, 0:1], min_val=0, max_val=1) != 0):
                    if pass_no == 0:
                        pool.memset(zero_rows[:, :], 0.0).then_inc(ge_zero_made, 1)
                        pool.iota(slot_index[:, :], pattern=[[P, TILES]], base=0, channel_multiplier=1
                                  ).then_inc(ge_index_set, 1)
                    pool.wait_ge(ge_cleared, pass_no + 1)
                    with_degree = pass_no == 0
                    puts = 2 if with_degree else 1
                    with pool.Fori(0, EW) as i:
                        pool.wait_ge(ge_index, i + (pass_no * EW + 1))
                        pool.sem_inc(pool_may_go, 1)
                        pool.indirect_dma_start(ge_msg[:, 0:width], None, table,
                                                bass.IndirectOffsetOnAxis(ge_src[:, :], axis=0),
                                                bounds_check=last_row, oob_is_err=False).then_inc(ge_fetched[pass_no], 16)
                        pool.indirect_dma_start(ge_cur[:, 0:width], None, sums,
                                                bass.IndirectOffsetOnAxis(ge_at[:, :], axis=0),
                                                bounds_check=last_row, oob_is_err=False).then_inc(ge_fetched[pass_no], 16)
                        if with_degree:
                            pool.indirect_dma_start(ge_deg[:, :], None, degree_dram,
                                                    bass.IndirectOffsetOnAxis(ge_at[:, :], axis=0),
                                                    bounds_check=N_PAD - 1, oob_is_err=False
                                                    ).then_inc(ge_fetched[pass_no], 16)
                        pool.wait_ge(ge_new_ready, i + (pass_no * EW + 1))
                        pool.sem_inc(pool_may_go, 1)
                        pool.indirect_dma_start(sums, bass.IndirectOffsetOnAxis(ge_put_at[:, :], axis=0),
                                                ge_new[:, 0:width], None,
                                                bounds_check=last_row, oob_is_err=False).then_inc(ge_put[pass_no], 16)
                        if with_degree:
                            pool.indirect_dma_start(degree_dram, bass.IndirectOffsetOnAxis(ge_put_at[:, :], axis=0),
                                                    ge_deg_new[:, :], None,
                                                    bounds_check=N_PAD - 1, oob_is_err=False).then_inc(ge_put[pass_no], 16)
                        pool.wait_ge(ge_put[pass_no], i * (16 * puts) + 16 * puts)
                        pool.sem_inc(pool_may_go, 1)
                    if pass_no == 0:
                        pool.wait_ge(ge_index_set, 1)

            def gathers(layer, table, width):
                def gather(s):
                    if not s.live():
                        return
                    if s.has(SLOTS):
                        pool.wait_ge(L0.nbr_split if layer is L0 else layer.summed, s.back(SLOTS).n + 1)
                    pool.wait_ge(layer.index_copied, s.n + 1)
                    pool.sem_inc(pool_may_go, 1)
                    for j in range(2):
                        pool.indirect_dma_start(nbr[s.slot][:, j, 0:width], None, table,
                                                bass.IndirectOffsetOnAxis(gather_at[s.slot][:, j:j + 1], axis=0),
                                                bounds_check=last_row, oob_is_err=False
                                                ).then_inc(layer.gathered[s.slot], 16)

                def step(s):
                    gather(s)
                    if layer is not L0:
                        return
                    t = s.back(8)
                    if t.live():
                        pool.wait_ge(L0.h1_hi_ready, t.n + 1)
                        if t.has(2):
                            pool.wait_ge(L0.dense_done, t.back(2).n + 1)
                        pool.sem_inc(pool_may_go, 1)
                        pool.tensor_tensor(hid_lo[t.half][:, :, :], h1[t.half][:, :, :],
                                           hid_hi[t.half][:, :, :].bitcast(FP32), ALU.subtract
                                           ).then_inc(L0.h1_lo_ready, 1)
                if layer is L0:
                    pipeline(pool, step, PAIRS, 8, rounds=3)
                else:
                    pipeline(pool, step, PAIRS, 0)

            def gather_pass(layer, pass_no):
                table, sums, width = GENERAL[pass_no]
                with pool.If(pool.value_load(general_flag[0:1, 0:1], min_val=0, max_val=1) != 0):
                    gathers(layer, sums, width)
                with pool.Else():
                    gathers(layer, table, width)

            pool.wait_ge(flag_set, 1)
            pool.wait_ge(tables_ready, 1)
            for q in range(SLOTS):
                pool.memset(nbr[q][:, :, :], 0.0).then_inc(nbr_cleared, 1)
            pool.wait_ge(nbr_cleared, SLOTS)
            for q in range(SLOTS):
                pool.memset(nbr[q][:, :, D:D + 1], 1.0).then_inc(nbr_cleared, 1)
            all_stored(pool, h0_stored, GROUPS // NORM_SLOTS)
            general(0)
            gather_pass(L0, 0)
            all_stored(pool, L0.stored, 2 * SLOT_USES)
            general(1)
            gather_pass(L1, 1)
            all_stored(pool, L1.stored, 2 * SLOT_USES)
            general(2)
            gather_pass(L2, 2)

        @block.scalar
        def _(act):
            act.wait_ge(const_made, 1)
            act.wait_ge(w_loaded, 16 * 7)
            act.activation(w_hi[:, :, :], weights[:, :, :], ACT.Copy).then_inc(w_hi_ready, 1)

            def norm_step(s):
                if s.live():
                    act.wait_ge(moments_ready, s.n + 1)
                    act.activation(std[s.slot][:, :], moments[s.slot][:, :, 1], ACT.Sqrt, bias=eps_col[:, :]
                                   ).then_inc(std_ready, 1)
                t = s.back(1)
                if t.live():
                    act.wait_ge(norm_ready, t.n + 1)
                    for j in range(4):
                        last = act.activation(norm_rows[t.slot][:, j, :], norm_rows[t.slot][:, j, :], ACT.Relu,
                                              bias=shift[t.slot][:, j:j + 1], scale=rstd[t.slot][:, j:j + 1])
                    last.then_inc(h0_ready, 1)
                u = s.back(2)
                if u.live():
                    act.wait_ge(h0_ready, u.n + 1)
                    act.dma_start(group_rows(h0_dram, u), norm_rows[u.slot][:, :, :]).then_inc(h0_stored[u.slot], 16)
            pipeline(act, norm_step, GROUPS, 2, slots=NORM_SLOTS)

            def nbr_hi_part(layer, s, tiles, width):
                if not s.live():
                    return
                act.wait_ge(layer.gathered[s.slot], (s.use + 1) * 32)
                if s.has(2):
                    act.wait_ge(layer.summed, s.back(2).n + 1)
                act.activation(nbr_hi[s.half][:, 0:tiles, 0:width], nbr[s.slot][:, 0:tiles, 0:width], ACT.Copy
                               ).then_inc(layer.nbr_hi_ready, 1)

            def layer0(first):
                nbr_hi_part(L0, first, 2, H)
                s = first.back(2)
                if s.live():
                    act.wait_ge(L0.own_loaded[s.slot], (s.use + 1) * 16)
                    act.wait_ge(L0.scale_ready, s.n + 1)
                    if s.has(2):
                        act.wait_ge(L0.agg_ready, s.back(2).n + 1)
                    for j in range(2):
                        last = act.activation(own_scaled[s.half][:, j, :], own[s.slot][:, j, 0:D], ACT.Copy,
                                              scale=self_scale[:, bass.ds(s.n * 2 + j, 1)])
                    last.then_inc(L0.own_scaled, 1)
                t = first.back(6)
                if t.live():
                    act.wait_ge(L0.dense_done, t.n + 1)
                    if t.has(SLOTS):
                        act.wait_ge(L0.stored[t.slot], t.use * 32)
                    for j in range(2):
                        last = act.activation(p_out[t.slot][:, j, :], out_bank(j)[:, 0:H], ACT.Copy)
                    last.then_inc(L0.p_ready, 1)
                t = first.back(3)
                if t.live():
                    act.wait_ge(L0.turned, t.n + 1)
                    if t.has(2):
                        act.wait_ge(L0.hid_done, t.back(2).n + 1)
                    act.activation(cat_hi[t.half][:, :, :], ps["turn"][t.half][:, :].rearrange("p (k n) -> p k n", k=2),
                                   ACT.Copy).then_inc(L0.hi_ready, 1)
                u = first.back(8)
                if u.live():
                    act.wait_ge(L0.rows_ready, u.n + 1)
                    act.dma_start(pair_rows(p_dram, u), p_out[u.slot][:, :, :]).then_inc(L0.stored[u.slot], 16)
                    act.dma_start(pair_rows(q_dram, u), q_out[u.slot][:, :, :]).then_inc(L0.stored[u.slot], 16)
                t = first.back(4)
                if t.live():
                    act.wait_ge(L0.hid_done, t.n + 1)
                    if t.has(2):
                        act.wait_ge(L0.h1_lo_ready, t.back(2).n + 1)
                    for m in range(2):
                        last = act.activation(h1[t.half][:, m, :], ps["hid"][t.half][:, m * PAIR:(m + 1) * PAIR],
                                              ACT.Relu, bias=b0_col[:, m:m + 1])
                    last.then_inc(L0.h1_made, 1)
            act.wait_ge(nbr_cleared, 2 * SLOTS)
            pipeline(act, layer0, PAIRS, 8, rounds=3)

            def layer1(first):
                if first.live():
                    if first.has(2):
                        act.wait_ge(L1.selected, first.back(2).n + 1)
                    for j in range(2):
                        last = act.activation(distance[first.half][:, j, :], iota_row[:, :], ACT.Abs, scale=-1.0,
                                              bias=slot_node[:, bass.ds(first.n * 2 + j, 1)])
                    last.then_inc(L1.distance_made, 1)
                nbr_hi_part(L1, first, L1_SPLIT, H)
                if first.live():
                    act.wait_ge(L1.distance_made, first.n + 1)
                    if first.has(2):
                        act.wait_ge(L1.summed, first.back(2).n + 1)
                    act.activation(select[first.half][:, :, :], distance[first.half][:, :, :], ACT.Relu, scale=-1.0,
                                   bias=ones[:, 0:1]).then_inc(L1.selected, 1)
                t = first.back(5)
                if t.live():
                    act.wait_ge(L1.dense_done, t.n + 1)
                    if t.has(SLOTS):
                        act.wait_ge(L1.stored[t.slot], t.use * 32)
                    act.activation(z_out[t.slot][:, :, :],
                                   ps["out"][t.half][:, :].rearrange("p (j f) -> p j f", j=2)[:, :, 0:D],
                                   ACT.Copy).then_inc(L1.z_ready, 1)
                t = first.back(3)
                if t.live():
                    act.wait_ge(L1.turned, t.n + 1)
                    if t.has(2):
                        act.wait_ge(L1.dense_done, t.back(2).n + 1)
                    act.activation(hid_hi[t.half][:, :, :], ps["turn"][t.half][:, :].rearrange("p (k n) -> p k n", k=2),
                                   ACT.Relu).then_inc(L1.hi_ready, 1)
            pipeline(act, layer1, PAIRS, 5, rounds=3)

            def layer2(s):
                u = s.back(1)
                if u.live():
                    act.wait_ge(L2.rows_ready, u.n + 1)
                    act.dma_start(pair_rows(out, u), y_out[u.slot][:, :, :]).then_inc(L2.stored[u.slot], 16)
            pipeline(act, layer2, PAIRS, 1)

        @block.vector
        def _(dve):
            dve.wait_ge(iota_made, 3)
            dve.tensor_copy(iota_row[:, :], iota_row_i[:, :])
            dve.tensor_copy(iota_col[:, :], iota_col_i[:, :])
            dve.tensor_copy(tile_base[:, :], tile_base_i[:, :])
            dve.memset(ones[:, :], 1.0)
            dve.memset(faults[:, :], 0.0)
            dve.memset(base_degree[:, :], 1.0)
            dve.memset(eps_col[:, :], EPS).then_inc(const_made, 1)
            dve.wait_ge(const_made, 1)
            dve.tensor_scalar(ident[:, :], iota_row[:, :], iota_col[:, 0:1], None, op0=ALU.is_equal
                              ).then_inc(const_made, 1)
            done = [0]

            def own_step(ins):
                done[0] += 1
                ins.then_inc(prep, 1)
                dve.wait_ge(prep, done[0])

            dve.wait_ge(dst_loaded, 32)
            dve.tensor_copy(samples[:, :], dst_all[:, :].rearrange("p (r w) -> p r w", w=ROW)[:, :, 0]
                            ).then_inc(sampled, 1)
            own_step(dve.tensor_tensor(scratch_rows[0:EP, 0:EW - 1], dst_all[:, 0:EW - 1], dst_all[:, 1:EW],
                                       ALU.is_gt))
            dve.reduce_sum(faults[0:EP, 0:1], scratch_rows[0:EP, 0:EW - 1], AX.X)
            own_step(dve.tensor_tensor(faults[0:EP - 1, 1:2], dst_all[0:EP - 1, EW - 1:EW], dst_next[:, 0:1], ALU.is_gt))

            dve.wait_ge(w_hi_ready, 1)
            dve.tensor_tensor(w_lo[:, :, :], weights[:, :, :], w_hi[:, :, :].bitcast(FP32), ALU.subtract
                              ).then_inc(w_ready, 1)

            dve.wait_ge(sample_spread, 16)
            for c in range(CHUNKS):
                own_step(dve.tensor_scalar(scratch_rows[0:TP, :], samples_b[:, :], tile_base[:, c:c + 1], None,
                                           op0=ALU.is_lt, op1=ALU.add, accum_out=below[:, c:c + 1]))
            own_step(dve.tensor_scalar(row_f[:, :], below[:, :], -1.0, 0.0, op0=ALU.add, op1=ALU.max))
            for r in range(WROWS):
                last = dve.tensor_scalar(row_index[:, r, :], row_f[:, :], float(r), None, op0=ALU.add)
            last.then_inc(rows_found, 1)

            def norm_step(s):
                if s.live():
                    dve.wait_ge(x_loaded[s.slot], (s.use + 1) * 16)
                    for j in range(4):
                        last = dve.bn_stats(stats[s.slot][:, j, :], norm_rows[s.slot][:, j, :])
                    last.then_inc(stats_done, 1)
                t = s.back(1)
                if t.live():
                    dve.wait_ge(std_ready, t.n + 1)
                    if s.live():
                        dve.wait_ge(stats_done, s.n + 1)
                    dve.reciprocal(rstd[t.slot][:, :], std[t.slot][:, :]).then_inc(recip_done, 1)
                if s.live():
                    if not t.live():
                        dve.wait_ge(stats_done, s.n + 1)
                    for j in range(4):
                        last = dve.bn_aggr(moments[s.slot][:, j, :], stats[s.slot][:, j, :])
                    last.then_inc(moments_ready, 1)
                if t.live():
                    dve.wait_ge(recip_done, t.n + 1)
                    dve.scalar_tensor_tensor(shift[t.slot][:, :], moments[t.slot][:, :, 0], -1.0, rstd[t.slot][:, :],
                                             op0=ALU.mult, op1=ALU.mult).then_inc(norm_ready, 1)
            peeled(norm_step, 0, 2 * NORM_SLOTS, GROUPS, NORM_SLOTS)
            looped(dve, norm_step, 2, NORM_BEFORE_KEYS, GROUPS, NORM_SLOTS)

            wide = [TP, CHUNKS, WIN]
            base_b = tile_base[:, :].rearrange("p (c a) -> p c a", a=1).to_broadcast(wide)
            dve.wait_ge(win_gathered, 16 * CHUNKS * WROWS * 2)
            dve.tensor_copy(wf_dst[:, :, :], win_dst[:, :, :])
            own_step(dve.tensor_copy(wf_src[:, :, :], win_src[:, :, :]))
            own_step(dve.tensor_tensor(wf_rel[:, :, :], wf_dst[:, :, :], base_b, ALU.subtract))
            own_step(dve.tensor_scalar(wf_in[:, :, :], wf_rel[:, :, :], 0.0, None, op0=ALU.is_ge))
            own_step(dve.scalar_tensor_tensor(wf_in[:, :, :], wf_rel[:, :, :], float(P), wf_in[:, :, :],
                                              op0=ALU.is_lt, op1=ALU.mult))
            dve.memset(wf_loop[:, :, WIN - 1:WIN], 0.0)
            own_step(dve.tensor_tensor(wf_loop[:, :, 0:WIN - 1], wf_dst[:, :, 0:WIN - 1], wf_dst[:, :, 1:WIN],
                                       ALU.not_equal))
            own_step(dve.tensor_tensor(wf_key[:, :, :], wf_src[:, :, :], wf_dst[:, :, :], ALU.is_equal))
            own_step(dve.tensor_tensor(wf_loop[:, :, :], wf_loop[:, :, :], wf_key[:, :, :], ALU.mult))
            own_step(dve.tensor_tensor(wf_loop[:, :, :], wf_loop[:, :, :], wf_in[:, :, :], ALU.mult))
            dve.reduce_sum(loop_count[:, :], wf_loop[:, :, :], AX.X)
            own_step(dve.tensor_tensor(wf_in[:, :, :], wf_in[:, :, :], wf_loop[:, :, :], ALU.subtract))
            own_step(dve.scalar_tensor_tensor(wf_key[:, :, :], wf_src[:, :, :], float(P), wf_rel[:, :, :],
                                              op0=ALU.mult, op1=ALU.add))
            own_step(dve.scalar_tensor_tensor(wf_key[:, :, :], wf_key[:, :, :], 1.0, wf_in[:, :, :],
                                              op0=ALU.add, op1=ALU.mult))
            own_step(dve.tensor_scalar(nodes_in[:, :], tile_base[:, :], -1.0, float(N_NODES), op0=ALU.mult, op1=ALU.add))
            own_step(dve.tensor_scalar(nodes_in[:, :], nodes_in[:, :], 0.0, float(P), op0=ALU.max, op1=ALU.min))
            own_step(dve.tensor_tensor(nodes_in[:, :], nodes_in[:, :], loop_count[:, :], ALU.not_equal))
            dve.reduce_sum(faults[0:TP, 2:3], nodes_in[:, :], AX.X)
            own_step(dve.tensor_scalar(below[:, :], wf_rel[:, :, WIN - 1], float(P), None, op0=ALU.is_lt))
            own_step(dve.reduce_sum(faults[0:TP, 3:4], below[:, :], AX.X))

            picked = done[0]
            with dve.Fori(NORM_BEFORE_KEYS, NORM_AFTER_KEYS) as i:
                r = i - NORM_BEFORE_KEYS
                for c in range(CHUNKS):
                    last = dve.max(top8[:, c, :], wf_key[:, c, :])
                last.then_inc(prep, 1)
                dve.wait_ge(prep, r * 2 + (picked + 1))
                dve.tensor_copy(keys[:, :, bass.ds(r * 8, 8)], top8[:, :, :])
                for c in range(CHUNKS):
                    last = dve.match_replace(wf_key[:, c, :], top8[:, c, :], wf_key[:, c, :], 0.0)
                last.then_inc(prep, 1)
                dve.wait_ge(prep, r * 2 + (picked + 2))
                dve.sem_inc(keys_ready, 1)
                for slot in range(NORM_SLOTS):
                    norm_step(Step(i, slot, GROUPS, True, NORM_SLOTS))
            done[0] += 2 * (P // 8)
            dve.reduce_max(faults[0:TP, 4:5], wf_key[:, :, :], AX.XY).then_inc(faults_ready, 1)
            dve.wait_ge(keys_turned, 1)
            own_step(dve.tensor_copy(keys_t[:, 0:4 * TP], ps["turn"][0][:, 0:4 * TP]))
            own_step(dve.tensor_copy(keys_t[:, 4 * TP:TILES], ps["turn"][1][:, 0:(CHUNKS - 4) * TP]))
            dve.tensor_scalar(key_i[:, :], keys_t[:, :], -1.0, None, op0=ALU.add)
            own_step(dve.tensor_scalar(empty_t[:, :], keys_t[:, :], 0.0, -float(SENTINEL), op0=ALU.is_equal,
                                       op1=ALU.mult))
            dve.tensor_scalar(slot_index[:, :], key_i[:, :], 7, None, op0=ALU.logical_shift_right)
            own_step(dve.tensor_scalar(node_i[:, :], key_i[:, :], P - 1, None, op0=ALU.bitwise_and))
            own_step(dve.tensor_tensor(slot_node[:, :], node_i[:, :], empty_t[:, :], ALU.add))
            dve.wait_ge(faults_summed, 1)
            own_step(dve.reduce_sum(fault_sum[:, :], ps["out"][0][:, 0:8], AX.X))
            dve.tensor_scalar(fast[:, :], fault_sum[:, :], 0.0, None, op0=ALU.is_equal)
            own_step(dve.tensor_scalar(general_flag[:, :], fault_sum[0:1, :], 0.0, None, op0=ALU.is_gt))
            dve.sem_inc(flag_set, 1)
            dve.sem_inc(tables_ready, 1)

            looped(dve, norm_step, NORM_AFTER_KEYS, GROUPS // NORM_SLOTS, GROUPS, NORM_SLOTS)
            peeled(norm_step, GROUPS, GROUPS + 1, GROUPS, NORM_SLOTS)

            def general(pass_no):
                table, sums, width = GENERAL[pass_no]
                with dve.If(dve.value_load(general_flag[0:1, 0:1], min_val=0, max_val=1) != 0):
                    with_degree = pass_no == 0
                    first = pass_no * EW
                    if with_degree:
                        dve.wait_ge(ge_loaded, 16)
                        dve.tensor_scalar(ge_before[:, :], iota_row[0:EP, 0:EP], iota_col[0:EP, :], None,
                                          op0=ALU.is_lt)
                    steps = 6
                    own = [0]
                    with dve.Fori(0, EW) as i:
                        def mine(ins):
                            own[0] += 1
                            ins.then_inc(ge_dve, 1)
                            dve.wait_ge(ge_dve, i * steps + (first * steps + own[0]))
                        column = dst_all[:, bass.ds(i, 1)]
                        dve.tensor_copy(ge_src[:, :], src_all[:, bass.ds(i, 1)])
                        dve.tensor_copy(ge_at[:, :], column)
                        mine(dve.tensor_copy(ge_dst[:, :], column))
                        dve.tensor_scalar(ge_dst_b[:, :], iota_row[0:EP, 0:EP], 0.0, ge_dst[:, :], op0=ALU.mult,
                                          op1=ALU.add).then_inc(ge_spread, 1)
                        dve.wait_ge(ge_turned, i + (first + 1))
                        mine(dve.tensor_scalar(ge_same[:, :], ps["hid"][1][0:EP, 0:EP], ge_dst[:, :], None,
                                               op0=ALU.is_equal))
                        dve.reduce_sum(ge_count[:, :], ge_same[:, :], AX.X)
                        mine(dve.tensor_tensor(ge_mask[:, :], ge_same[:, :], ge_before[:, :], ALU.mult))
                        mine(dve.reduce_sum(ge_dup[:, :], ge_mask[:, :], AX.X))
                        mine(dve.tensor_scalar(ge_dup[:, :], ge_dup[:, :], 0.0, float(SENTINEL), op0=ALU.is_gt,
                                               op1=ALU.mult))
                        mine(dve.tensor_tensor(ge_put_at[:, :], ge_dst[:, :], ge_dup[:, :], ALU.add))
                        dve.sem_inc(ge_index, 1)
                        dve.wait_ge(ge_summed, i + (first + 1))
                        fetches = 3 if with_degree else 2
                        dve.wait_ge(ge_fetched[pass_no], i * (16 * fetches) + 16 * fetches)
                        if with_degree:
                            dve.tensor_tensor(ge_deg_new[:, :], ge_deg[:, :], ge_count[:, :], ALU.add)
                        dve.tensor_tensor(ge_new[:, 0:width], ps["hid"][0][0:EP, 0:width], ge_cur[:, 0:width],
                                          ALU.add).then_inc(ge_new_ready, 1)
                        puts = 2 if with_degree else 1
                        dve.wait_ge(ge_put[pass_no], i * (16 * puts) + 16 * puts)
                    if with_degree:
                        dve.wait_ge(ge_base_loaded, 16)
                        dve.wait_ge(ge_index_set, 1)
                        dve.tensor_scalar(base_degree[:, :], ge_base[:, :], 1.0, None, op0=ALU.max)
                        dve.tensor_scalar(slot_node[:, :], ge_base[:, :], 0.0, iota_col[:, :], op0=ALU.mult,
                                          op1=ALU.add).then_inc(ge_nodes_set, 1)
                        dve.wait_ge(ge_nodes_set, 1)

            def copies_index(layer, s):
                if not s.live():
                    return
                if s.has(SLOTS):
                    dve.wait_ge(layer.gathered[s.slot], s.use * 32)
                dve.tensor_copy(gather_at[s.slot][:, :], slot_index[:, bass.ds(s.n * 2, 2)]
                                ).then_inc(layer.index_copied, 1)

            def selects(layer, s):
                if not s.live():
                    return
                if s.has(2):
                    dve.wait_ge(layer.summed, s.back(2).n + 1)
                for j in range(2):
                    last = dve.tensor_scalar(select[s.half][:, j, :], iota_row[:, :],
                                             slot_node[:, bass.ds(s.n * 2 + j, 1)], None, op0=ALU.is_equal)
                last.then_inc(layer.selected, 1)

            def nbr_lo_part(layer, s, tiles, width):
                if not s.live():
                    return
                dve.wait_ge(layer.nbr_hi_ready, s.n + 1)
                if s.has(2):
                    dve.wait_ge(layer.summed, s.back(2).n + 1)
                dve.tensor_tensor(nbr_lo[s.half][:, 0:tiles, 0:width], nbr[s.slot][:, 0:tiles, 0:width],
                                  nbr_hi[s.half][:, 0:tiles, 0:width].bitcast(FP32), ALU.subtract
                                  ).then_inc(layer.nbr_split, 1)

            def means(layer, s, width, added):
                dve.wait_ge(layer.summed, s.n + 1)
                if s.has(2):
                    dve.wait_ge(layer.turned, s.back(2).n + 1)
                for j in range(2):
                    last = dve.scalar_tensor_tensor(agg[s.half][:, j, 0:width],
                                                    sum_bank(layer, s)[:, j * H:j * H + width],
                                                    inv_degree[:, bass.ds(s.n * 2 + j, 1)],
                                                    added[:, j, 0:width], op0=ALU.mult, op1=ALU.add)
                last.then_inc(layer.agg_ready, 1)

            general(0)

            def layer0(first):
                copies_index(L0, first)
                t = first.back(11)
                if t.live():
                    dve.wait_ge(L0.p_ready, t.n + 1)
                    if t.has(2):
                        dve.wait_ge(L0.rows_ready, t.back(2).n + 1)
                    for j in range(2):
                        last = dve.tensor_tensor(q_part[t.half][:, j, :], out_bank(j)[:, H:2 * H], b1_rows[:, :],
                                                 ALU.add)
                    last.then_inc(L0.q_part_ready, 1)
                t = first.back(8)
                if t.live():
                    dve.wait_ge(L0.hi_ready, t.n + 1)
                    if t.has(2):
                        dve.wait_ge(L0.hid_done, t.back(2).n + 1)
                    dve.tensor_tensor(cat_lo[t.half][:, :, :], ps["turn"][t.half][:, :].rearrange("p (k n) -> p k n", k=2),
                                      cat_hi[t.half][:, :, :].bitcast(FP32), ALU.subtract).then_inc(L0.lo_ready, 1)
                selects(L0, first.back(4))
                t = first.back(11)
                if t.live():
                    dve.wait_ge(L0.q_part_ready, t.n + 1)
                    if t.has(SLOTS):
                        dve.wait_ge(L0.stored[t.slot], t.use * 32)
                    for j in range(2):
                        last = dve.scalar_tensor_tensor(q_out[t.slot][:, j, :], p_out[t.slot][:, j, :],
                                                        self_scale[:, bass.ds(t.n * 2 + j, 1)], q_part[t.half][:, j, :],
                                                        op0=ALU.mult, op1=ALU.add)
                    last.then_inc(L0.rows_ready, 1)
                nbr_lo_part(L0, first.back(4), 2, H)
                s = first.back(5)
                if s.live():
                    dve.wait_ge(L0.summed, s.n + 1)
                    two = bass.ds(s.n * 2, 2)
                    counts = sum_bank(L0, s).rearrange("p (j f) -> p j f", j=2)[:, :, D]
                    dve.scalar_tensor_tensor(degree[s.half][:, :], counts, fast[:, :], base_degree[:, two],
                                             op0=ALU.mult, op1=ALU.add).then_inc(L0.degree_done, 1)
                t = s.back(4)
                if t.live():
                    dve.wait_ge(L0.h1_made, t.n + 1)
                    if t.has(2):
                        dve.wait_ge(L0.dense_done, t.back(2).n + 1)
                    dve.tensor_copy(hid_hi[t.half][:, :, :], h1[t.half][:, :, :]).then_inc(L0.h1_hi_ready, 1)
                if s.live():
                    dve.wait_ge(L0.degree_done, s.n + 1)
                    dve.reciprocal(inv_degree[:, two], degree[s.half][:, :]).then_inc(L0.recip_done, 1)
                if s.live():
                    dve.wait_ge(L0.recip_done, s.n + 1)
                    dve.tensor_scalar(self_scale[:, two], inv_degree[:, two], fast[:, :], None, op0=ALU.mult
                                      ).then_inc(L0.scale_ready, 1)
                t = s.back(1)
                if t.live():
                    dve.wait_ge(L0.own_scaled, t.n + 1)
                    means(L0, t, D, own_scaled[t.half])
            dve.wait_ge(nbr_cleared, 2 * SLOTS)
            dve.wait_ge(bias_loaded, 32)
            pipeline(dve, layer0, PAIRS, 11, rounds=4)

            general(1)

            def layer1(first):
                copies_index(L1, first)
                nbr_lo_part(L1, first.back(4), L1_SPLIT, H)
                s = first.back(5)
                t = s.back(2)
                if t.live():
                    dve.wait_ge(L1.hi_ready, t.n + 1)
                    if t.has(2):
                        dve.wait_ge(L1.dense_done, t.back(2).n + 1)
                    dve.scalar_tensor_tensor(hid_lo[t.half][:, :, :],
                                             ps["turn"][t.half][:, :].rearrange("p (k n) -> p k n", k=2), 0.0,
                                             hid_hi[t.half][:, :, :].bitcast(FP32), op0=ALU.max, op1=ALU.subtract
                                             ).then_inc(L1.lo_ready, 1)
                t = s.back(4)
                if t.live():
                    dve.wait_ge(L1.z_ready, t.n + 1)
                    if t.has(SLOTS):
                        dve.wait_ge(L1.stored[t.slot], t.use * 32)
                    for j in range(2):
                        last = dve.scalar_tensor_tensor(y_out[t.slot][:, j, :], z_out[t.slot][:, j, :],
                                                        self_scale[:, bass.ds(t.n * 2 + j, 1)],
                                                        ps["out"][t.half][:, j * H + D:(j + 1) * H],
                                                        op0=ALU.mult, op1=ALU.add)
                    last.then_inc(L1.rows_ready, 1)
                if s.live():
                    dve.wait_ge(L1.own_loaded[s.slot], (s.use + 1) * 16)
                    means(L1, s, H, own[s.slot])
            pipeline(dve, layer1, PAIRS, 9, rounds=4)

            general(2)

            def layer2(first):
                copies_index(L2, first)
                selects(L2, first.back(4))
                s = first.back(5)
                if s.live():
                    dve.wait_ge(L2.own_loaded[s.slot], (s.use + 1) * 16)
                    dve.wait_ge(L2.summed, s.n + 1)
                    if s.has(2):
                        dve.wait_ge(L2.rows_ready, s.back(2).n + 1)
                    for j in range(2):
                        last = dve.scalar_tensor_tensor(y_plus_sums[s.half][:, j, :],
                                                        sum_bank(L2, s)[:, j * H:j * H + D],
                                                        inv_degree[:, bass.ds(s.n * 2 + j, 1)],
                                                        own[s.slot][:, j, 0:D], op0=ALU.mult, op1=ALU.add)
                    dve.wait_ge(L2.x_loaded[s.slot], (s.use + 1) * 16)
                    dve.tensor_tensor(x_plus_b2[s.half][:, :, :], x_in[s.slot][:, :, :],
                                      b2_rows[:, :].rearrange("p (a f) -> p a f", a=1).to_broadcast([P, 2, D]),
                                      ALU.add).then_inc(L2.y_added, 1)
                t = s.back(1)
                if t.live():
                    dve.wait_ge(L2.y_added, t.n + 1)
                    if t.has(SLOTS):
                        dve.wait_ge(L2.stored[t.slot], t.use * 16)
                    dve.tensor_tensor(y_out[t.slot][:, :, :], y_plus_sums[t.half][:, :, :], x_plus_b2[t.half][:, :, :],
                                      ALU.add).then_inc(L2.rows_ready, 1)
            pipeline(dve, layer2, PAIRS, 6, rounds=3)

        @block.tensor
        def _(pe):
            pe.wait_ge(const_made, 2)
            pe.wait_ge(keys_ready, P // 8)
            for c in range(CHUNKS):
                at = (c % 4) * TP
                last = nc.tensor.matmul(ps["turn"][c // 4][:, at:at + TP], keys[:, c, :], ident[0:TP, 0:TP],
                                        is_transpose=True, start=True, stop=True)
            last.then_inc(keys_turned, 1)
            pe.wait_ge(faults_ready, 1)
            nc.tensor.matmul(ps["out"][0][:, 0:8], ones[:, :], faults[:, :], start=True, stop=True
                             ).then_inc(faults_summed, 1)

            def general(pass_no):
                table, sums, width = GENERAL[pass_no]
                with pe.If(pe.value_load(general_flag[0:1, 0:1], min_val=0, max_val=1) != 0):
                    with_degree = pass_no == 0
                    fetches = 3 if with_degree else 2
                    first = pass_no * EW
                    with pe.Fori(0, EW) as i:
                        pe.wait_ge(ge_spread, i + (first + 1))
                        nc.tensor.matmul(ps["hid"][1][0:EP, 0:EP], ge_dst_b[:, :], ident[0:EP, 0:EP],
                                         is_transpose=True, start=True, stop=True).then_inc(ge_turned, 1)
                        pe.wait_ge(ge_index, i + (first + 1))
                        pe.wait_ge(ge_fetched[pass_no], i * (16 * fetches) + 16 * fetches)
                        nc.tensor.matmul(ps["hid"][0][0:EP, 0:width], ge_same[:, :], ge_msg[:, 0:width],
                                         start=True, stop=True).then_inc(ge_summed, 1)
                    pe.wait_ge(ge_new_ready, first + EW)

            def sums(layer, s, width, split):
                if not s.live():
                    return
                if split:
                    pe.wait_ge(layer.nbr_split, s.n + 1)
                if split < 2:
                    pe.wait_ge(layer.gathered[s.slot], (s.use + 1) * 32)
                pe.wait_ge(layer.selected, s.n + 1)
                banks = 2 if layer is L0 else SLOTS
                if s.has(banks):
                    pe.wait_ge(layer.y_added if layer is L2 else layer.agg_ready, s.back(banks).n + 1)
                for j in range(2):
                    o = sum_bank(layer, s)[:, j * H:j * H + width]
                    if j < split:
                        nc.tensor.matmul(o, select[s.half][:, j, :], nbr_hi[s.half][:, j, 0:width],
                                         start=True, stop=False)
                        last = nc.tensor.matmul(o, select[s.half][:, j, :], nbr_lo[s.half][:, j, 0:width],
                                                start=False, stop=True)
                    else:
                        last = nc.tensor.matmul(o, select[s.half][:, j, :].bitcast(FP32), nbr[s.slot][:, j, 0:width],
                                                start=True, stop=True)
                last.then_inc(layer.summed, 1)

            pe.wait_ge(w_ready, 1)
            pe.wait_ge(flag_set, 1)
            pe.wait_ge(nbr_cleared, 2 * SLOTS)
            general(0)

            def product(o, pairs):
                terms = [t for (a_hi, a_lo), (b_hi, b_lo) in pairs
                         for t in ((a_hi, b_hi), (a_hi, b_lo), (a_lo, b_hi))]
                for n, (a, b) in enumerate(terms):
                    ins = nc.tensor.matmul(o, a, b, start=n == 0, stop=n == len(terms) - 1)
                return ins

            def layer0(s):
                sums(L0, s, H, 2)
                t = s.back(5)
                if t.live():
                    pe.wait_ge(L0.h1_lo_ready, t.n + 1)
                    if t.has(1):
                        pe.wait_ge(L0.p_ready, t.back(1).n + 1)
                        pe.wait_ge(L0.q_part_ready, t.back(1).n + 1)
                    for j in range(2):
                        nodes = slice(j * P, (j + 1) * P)
                        last = product(out_bank(j), [
                            ((hid_hi[t.half][:, m, nodes], hid_lo[t.half][:, m, nodes]),
                             tuple(w[:, W1 + 2 * m:W1 + 2 * m + 2, :].rearrange("p t n -> p (t n)") for w in (w_hi, w_lo)))
                            for m in range(2)])
                    last.then_inc(L0.dense_done, 1)
                t = s.back(2)
                if t.live():
                    pe.wait_ge(L0.agg_ready, t.n + 1)
                    pe.wait_ge(L0.own_loaded[t.slot], (t.use + 1) * 16)
                    if t.has(2):
                        pe.wait_ge(L0.lo_ready, t.back(2).n + 1)
                    for j in range(2):
                        for k, rows in enumerate((own[t.slot], agg[t.half])):
                            at = k * PAIR + j * P
                            last = nc.tensor.matmul(ps["turn"][t.half][:, at:at + P], rows[:, j, 0:D], ident[:, :],
                                                    is_transpose=True, start=True, stop=True)
                    last.then_inc(L0.turned, 1)
                t = s.back(3)
                if t.live():
                    pe.wait_ge(L0.lo_ready, t.n + 1)
                    if t.has(2):
                        pe.wait_ge(L0.h1_made, t.back(2).n + 1)
                    for m in range(2):
                        out_features = slice(m * P, (m + 1) * P)
                        last = product(ps["hid"][t.half][:, m * PAIR:(m + 1) * PAIR],
                                       [((w_hi[:, W0 + k, out_features], w_lo[:, W0 + k, out_features]),
                                         (cat_hi[t.half][:, k, :], cat_lo[t.half][:, k, :])) for k in range(2)])
                    last.then_inc(L0.hid_done, 1)
            pipeline(pe, layer0, PAIRS, 5)

            general(1)

            def layer1(s):
                sums(L1, s, H, L1_SPLIT)
                t = s.back(3)
                if t.live():
                    pe.wait_ge(L1.lo_ready, t.n + 1)
                    if t.has(2):
                        pe.wait_ge(L1.z_ready, t.back(2).n + 1)
                        pe.wait_ge(L1.rows_ready, t.back(2).n + 1)
                    for j in range(2):
                        o = ps["out"][t.half][:, j * H:(j + 1) * H]
                        nodes = slice(j * P, (j + 1) * P)
                        last = product(o, [((hid_hi[t.half][:, m, nodes], hid_lo[t.half][:, m, nodes]),
                                            (w_hi[:, W2 + m, :], w_lo[:, W2 + m, :])) for m in range(2)])
                    last.then_inc(L1.dense_done, 1)
                t = s.back(1)
                if t.live():
                    pe.wait_ge(L1.agg_ready, t.n + 1)
                    if t.has(2):
                        pe.wait_ge(L1.lo_ready, t.back(2).n + 1)
                    for m in range(2):
                        for j in range(2):
                            at = m * PAIR + j * P
                            last = nc.tensor.matmul(ps["turn"][t.half][:, at:at + P], agg[t.half][:, j, m * P:(m + 1) * P],
                                                    ident[:, :], is_transpose=True, start=True, stop=True)
                    last.then_inc(L1.turned, 1)
            pipeline(pe, layer1, PAIRS, 3)

            general(2)
            pipeline(pe, lambda s: sums(L2, s, D, 0), PAIRS, 0)


INPUTS = ["x", "src", "dst", "L0_gnn_ws0", "L0_gnn_wn0", "L0_gnn_b0", "L0_gnn_ws1", "L0_gnn_wn1", "L0_gnn_b1",
          "L0_gnn_ws2", "L0_gnn_wn2", "L0_gnn_b2"]


def kernel(**inputs):
    import numpy as np
    import concourse.bacc as bacc
    from concourse.bass_utils import run_bass_kernel_spmd

    nc = bacc.Bacc("TRN2", target_bir_lowering=False, num_devices=1)
    arrays, args = {}, []
    for name in INPUTS:
        a = np.ascontiguousarray(inputs[name])
        if name == "x":
            padded = np.zeros((N_PAD, D), a.dtype)
            padded[:N_NODES] = a
            a = padded
        arrays[f"in_{name}"] = a
        args.append(nc.dram_tensor(f"in_{name}", a.shape, mybir.dt.from_np(a.dtype), kind="ExternalInput").ap())
    out = nc.dram_tensor("out_rows", (N_PAD, D), FP32, kind="ExternalOutput").ap()
    build(nc, *args, out)
    r = run_bass_kernel_spmd(nc, [arrays], core_ids=[0])
    return r.results[0]["out_rows"][:N_NODES]
```
